# Optimizing a Trainium2 kernel written in Bass

```python
import numpy as np
import jax
import jax.numpy as jnp

def _softmax(x, axis=-1):
    return jax.nn.softmax(x, axis=axis)
def _gelu(x):
    return jax.nn.gelu(x, approximate=True)
def _silu(x):
    return jax.nn.silu(x)
def _sigmoid(x):
    return jax.nn.sigmoid(x)
def _layernorm(x, axis=-1, eps=1e-5):
    m = jnp.mean(x, axis=axis, keepdims=True)
    v = jnp.var(x, axis=axis, keepdims=True)
    return (x - m) / jnp.sqrt(v + eps)
def _scatter_add(tgt, idx, src, axis=0):
    return tgt.at[idx].add(src)
def _segment_sum(src, seg, n):
    return jax.ops.segment_sum(src, seg, n)

kernel_name = 'mk_conv_seq_d2_conv_nchw96_679cf8'

def setup_inputs(seed: int = 0):
    np.random.seed(seed)
    _w = jnp.asarray
    def _rec_inputs():
        import jax
        import jax.numpy as jnp
        _gk = jax.random.key(seed)
        x = 7.572e-06 + 1 * jax.random.normal(jax.random.fold_in(_gk, 1), (32, 96, 56, 56), jnp.float32)
        return x
    x = _rec_inputs()
    def _L0_conv_setup():
        import jax, jax.numpy as jnp
        import numpy as np
        LN_EPS = 1e-05
        key = jax.random.key(seed)
        ks = jax.random.split(key, 8)
        dim, B, H, W = (96, 32, 56, 56)
        return {'x': jax.random.normal(ks[0], (B, dim, H, W), jnp.float32), 'conv_w': jax.random.normal(ks[1], (dim, 1, 7, 7), jnp.float32) * 0.05, 'conv_b': jax.random.normal(ks[2], (dim,), jnp.float32) * 0.05, 'ln_g': jnp.ones((dim,), jnp.float32), 'ln_b': jnp.zeros((dim,), jnp.float32), 'w1': jax.random.normal(ks[3], (dim, 4 * dim), jnp.float32) * 0.05, 'b1': jax.random.normal(ks[4], (4 * dim,), jnp.float32) * 0.05, 'w2': jax.random.normal(ks[5], (4 * dim, dim), jnp.float32) * 0.05, 'b2': jax.random.normal(ks[6], (dim,), jnp.float32) * 0.05, 'layer_scale': jnp.ones((dim, 1, 1), jnp.float32)}
    _L0_conv_all = _L0_conv_setup()
    _L0_conv_in = {k: v for k, v in _L0_conv_all.items() if k in ('conv_w', 'conv_b', 'ln_g', 'ln_b', 'w1', 'b1', 'w2', 'b2', 'layer_scale', )}
    del _L0_conv_all

    def _L1_conv_setup():
        import jax, jax.numpy as jnp
        import numpy as np
        B_SZ, D, H, W = (32, 96, 64, 64)
        N = 4
        R = 6
        K = 5
        EPS = 1e-09
        LOG_EPS = float(np.log(EPS))

        def _forward(x, conv_w, conv_b, x_proj_w, dt_w, dt_b, A_logs, Ds):
            B, C, h, w = x.shape
            L = h * w
            x = jax.lax.conv_general_dilated(x, conv_w, window_strides=(1, 1), padding=((K // 2, K // 2), (K // 2, K // 2)), dimension_numbers=('NCHW', 'OIHW', 'NCHW'), feature_group_count=C)
            x = x + conv_b[None, :, None, None]
            x = jax.nn.silu(x)
            xs = x.reshape(B, C, L)
            x_dbl = jnp.einsum('kd,bdl->bkl', x_proj_w, xs)
            dts, Bs, Cs = (x_dbl[:, :R], x_dbl[:, R:R + N], x_dbl[:, R + N:])
            delta = jax.nn.softplus(jnp.einsum('dr,brl->bdl', dt_w, dts) + dt_b[None, :, None])
            A = -jnp.exp(A_logs)
            log_dA = jnp.maximum(delta[:, :, None, :] * A[None, :, :, None], LOG_EPS)
            P = jnp.exp(jnp.cumsum(log_dA, axis=-1))
            dB_u = delta[:, :, None, :] * Bs[:, None, :, :] * xs[:, :, None, :]
            hs = P * jnp.cumsum(dB_u / jnp.maximum(P, EPS), axis=-1)
            y = jnp.einsum('bdnl,bnl->bdl', hs, Cs) + xs * Ds[None, :, None]
            return y.reshape(B, C, h, w)
        key = jax.random.key(seed)
        ks = jax.random.split(key, 8)
        x = jax.random.normal(ks[0], (B_SZ, D, H, W), dtype=jnp.float32)
        conv_w = jax.random.normal(ks[1], (D, 1, K, K), dtype=jnp.float32) * (1.0 / K)
        conv_b = jax.random.normal(ks[2], (D,), dtype=jnp.float32) * 0.02
        x_proj_w = jax.random.normal(ks[3], (R + 2 * N, D), dtype=jnp.float32) * D ** (-0.5)
        dt_w = jax.random.uniform(ks[4], (D, R), dtype=jnp.float32, minval=-R ** (-0.5), maxval=R ** (-0.5))
        dt = jnp.exp(jax.random.uniform(ks[5], (D,), dtype=jnp.float32) * (np.log(0.1) - np.log(0.001)) + np.log(0.001))
        dt = jnp.clip(dt, 0.0001, None)
        dt_b = dt + jnp.log(-jnp.expm1(-dt))
        A_logs = jnp.log(jnp.broadcast_to(jnp.arange(1, N + 1, dtype=jnp.float32), (D, N)))
        Ds = jnp.ones((D,), dtype=jnp.float32)
        return {'x': x, 'conv_w': conv_w, 'conv_b': conv_b, 'x_proj_w': x_proj_w, 'dt_w': dt_w, 'dt_b': dt_b, 'A_logs': A_logs, 'Ds': Ds}
    _L1_conv_all = _L1_conv_setup()
    _L1_conv_in = {k: v for k, v in _L1_conv_all.items() if k in ('conv_w', 'conv_b', 'x_proj_w', 'dt_w', 'dt_b', 'A_logs', 'Ds', )}
    del _L1_conv_all

    return {
        "x": x,
        "L0_conv_conv_w": _L0_conv_in["conv_w"],
        "L0_conv_conv_b": _L0_conv_in["conv_b"],
        "L0_conv_ln_g": _L0_conv_in["ln_g"],
        "L0_conv_ln_b": _L0_conv_in["ln_b"],
        "L0_conv_w1": _L0_conv_in["w1"],
        "L0_conv_b1": _L0_conv_in["b1"],
        "L0_conv_w2": _L0_conv_in["w2"],
        "L0_conv_b2": _L0_conv_in["b2"],
        "L0_conv_layer_scale": _L0_conv_in["layer_scale"],
        "L1_conv_conv_w": _L1_conv_in["conv_w"],
        "L1_conv_conv_b": _L1_conv_in["conv_b"],
        "L1_conv_x_proj_w": _L1_conv_in["x_proj_w"],
        "L1_conv_dt_w": _L1_conv_in["dt_w"],
        "L1_conv_dt_b": _L1_conv_in["dt_b"],
        "L1_conv_A_logs": _L1_conv_in["A_logs"],
        "L1_conv_Ds": _L1_conv_in["Ds"],
    }

def reference(x, L0_conv_conv_w, L0_conv_conv_b, L0_conv_ln_g, L0_conv_ln_b, L0_conv_w1, L0_conv_b1, L0_conv_w2, L0_conv_b2, L0_conv_layer_scale, L1_conv_conv_w, L1_conv_conv_b, L1_conv_x_proj_w, L1_conv_dt_w, L1_conv_dt_b, L1_conv_A_logs, L1_conv_Ds):
    import jax
    import jax.numpy as jnp
    def _L0_conv_ref(x, conv_w, conv_b, ln_g, ln_b, w1, b1, w2, b2, layer_scale):
        import jax, jax.numpy as jnp
        import numpy as np
        LN_EPS = 1e-05
        dim = x.shape[1]
        h = jax.lax.conv_general_dilated(x, conv_w, window_strides=(1, 1), padding=((3, 3), (3, 3)), dimension_numbers=('NCHW', 'OIHW', 'NCHW'), feature_group_count=dim)
        h = h + conv_b[None, :, None, None]
        h = jnp.transpose(h, (0, 2, 3, 1))
        mu = jnp.mean(h, axis=-1, keepdims=True)
        var = jnp.var(h, axis=-1, keepdims=True)
        h = (h - mu) * jax.lax.rsqrt(var + LN_EPS) * ln_g + ln_b
        h = jax.nn.gelu(jnp.einsum('bhwc,cf->bhwf', h, w1) + b1, approximate=False)
        h = jnp.einsum('bhwf,fc->bhwc', h, w2) + b2
        h = jnp.transpose(h, (0, 3, 1, 2)) * layer_scale[None]
        return h + x

    def _L1_conv_ref(x, conv_w, conv_b, x_proj_w, dt_w, dt_b, A_logs, Ds):
        import jax, jax.numpy as jnp
        import numpy as np
        B_SZ, D, H, W = (32, 96, 64, 64)
        N = 4
        R = 6
        K = 5
        EPS = 1e-09
        LOG_EPS = float(np.log(EPS))

        def _forward(x, conv_w, conv_b, x_proj_w, dt_w, dt_b, A_logs, Ds):
            B, C, h, w = x.shape
            L = h * w
            x = jax.lax.conv_general_dilated(x, conv_w, window_strides=(1, 1), padding=((K // 2, K // 2), (K // 2, K // 2)), dimension_numbers=('NCHW', 'OIHW', 'NCHW'), feature_group_count=C)
            x = x + conv_b[None, :, None, None]
            x = jax.nn.silu(x)
            xs = x.reshape(B, C, L)
            x_dbl = jnp.einsum('kd,bdl->bkl', x_proj_w, xs)
            dts, Bs, Cs = (x_dbl[:, :R], x_dbl[:, R:R + N], x_dbl[:, R + N:])
            delta = jax.nn.softplus(jnp.einsum('dr,brl->bdl', dt_w, dts) + dt_b[None, :, None])
            A = -jnp.exp(A_logs)
            log_dA = jnp.maximum(delta[:, :, None, :] * A[None, :, :, None], LOG_EPS)
            P = jnp.exp(jnp.cumsum(log_dA, axis=-1))
            dB_u = delta[:, :, None, :] * Bs[:, None, :, :] * xs[:, :, None, :]
            hs = P * jnp.cumsum(dB_u / jnp.maximum(P, EPS), axis=-1)
            y = jnp.einsum('bdnl,bnl->bdl', hs, Cs) + xs * Ds[None, :, None]
            return y.reshape(B, C, h, w)
        return _forward(x, conv_w, conv_b, x_proj_w, dt_w, dt_b, A_logs, Ds)

    def _gn(v, G=32, eps=1e-5):
        B_, C_, H_, W_ = v.shape
        g = v.reshape(B_, G, C_ // G, H_, W_)
        m = jnp.mean(g, axis=(2, 3, 4), keepdims=True)
        s = jnp.var(g, axis=(2, 3, 4), keepdims=True)
        return ((g - m) / jnp.sqrt(s + eps)).reshape(v.shape)

    def _ln_c(v, eps=1e-6):
        m = jnp.mean(v, axis=1, keepdims=True)
        s = jnp.var(v, axis=1, keepdims=True)
        return (v - m) / jnp.sqrt(s + eps)

    def _ln_t(v, eps=1e-5):
        m = jnp.mean(v, axis=-1, keepdims=True)
        s = jnp.var(v, axis=-1, keepdims=True)
        return (v - m) / jnp.sqrt(s + eps)

    def _to_tokens(v):
        B_, C_, H_, W_ = v.shape
        return v.reshape(B_, C_, H_ * W_).transpose(0, 2, 1)
    def _from_tokens(t, like):
        B_, C_, H_, W_ = like.shape
        return t.transpose(0, 2, 1).reshape(B_, C_, H_, W_)

    x = _L0_conv_ref(x, L0_conv_conv_w, L0_conv_conv_b, L0_conv_ln_g, L0_conv_ln_b, L0_conv_w1, L0_conv_b1, L0_conv_w2, L0_conv_b2, L0_conv_layer_scale)
    x = _L1_conv_ref(x, L1_conv_conv_w, L1_conv_conv_b, L1_conv_x_proj_w, L1_conv_dt_w, L1_conv_dt_b, L1_conv_A_logs, L1_conv_Ds)
    return x


_drawn_inputs = setup_inputs


def setup_inputs(seed=0):
    import zlib

    import numpy as np

    out = dict(_drawn_inputs(seed))
    spreads = {'L0_conv_ln_g': (1.0, 0.2),
     'L0_conv_ln_b': (0.0, 0.3),
     'L0_conv_layer_scale': (1.0, 0.2),
     'L1_conv_Ds': (1.0, 0.2)}
    factors = {'L1_conv_conv_b': 2.892, 'L1_conv_dt_w': 4.693}
    for name, (base, spread) in spreads.items():
        noise = np.random.default_rng([zlib.crc32(name.encode()), seed]).standard_normal(out[name].shape)
        drawn = base * np.exp(spread * noise) if base else spread * noise
        out[name] = jnp.asarray(drawn.astype(out[name].dtype))
    for name, factor in factors.items():
        out[name] = (out[name] * factor).astype(out[name].dtype)
    return out
```

```python
from contextlib import ExitStack

import numpy as np

import concourse.bass as bass
from concourse import mybir

F32 = mybir.dt.float32
BF16 = mybir.dt.bfloat16
ALU = mybir.AluOpType
ACT = mybir.ActivationFunctionType
AX_X = mybir.AxisListType.X
ds = bass.ds

IMAGES, C, H, W = 32, 96, 56, 56
L = H * W
GI = 4
GROUPS = IMAGES // GI
ROWS = 2
TOK = ROWS * W
IMG_BLK = H // ROWS
BLOCKS = GI * IMG_BLK
BLKS = 4
BT = BLKS * TOK
BANDS = L // BT
UNITS = GI * BANDS
BANK = 512
CQ = 4
QUNITS = C // CQ
TW = 4

K1, PAD1 = 7, 3
COLS1 = W + 2 * PAD1
WIN1 = ROWS * COLS1
KT1 = (ROWS + K1 - 1) // ROWS
NWIN1 = (H + 2 * PAD1) // ROWS
TURNS1 = -(-NWIN1 // TW)
SLOTS1 = 6
FF = 4 * C
FT = FF // 128
LN_EPS = 1e-5

K2, PAD2 = 5, 2
COLS2 = W + 2 * PAD2
WIN2 = ROWS * COLS2
KT2 = (ROWS + K2 - 1) // ROWS
NWIN2 = (H + 2 * PAD2) // ROWS
CB = 32
CBS = C // CB
TURNS2 = 2
TW2 = NWIN2 // TURNS2
SLOTS2 = 4
SLABS = 3
AHEAD = 10
ZSTEPS = 4
N, R = 4, 6
EPS = 1e-9
TILES = GI * C // 128
STEPS = TILES * N
BC = 2 * GI * N
XD = 3 * BC + GI * R


def window_copy(win, ps_stage, n):
    i, part = n // TURNS1, n % TURNS1
    a, z = part * TW, min((part + 1) * TW, NWIN1)
    return (win[:, :, i, a:z].rearrange("p c w -> p w c"),
            ps_stage[n % 2][0:WIN1, 0:(z - a) * C].rearrange("p (w c) -> p w c", c=C))


def layer0(nc, groups, x, t1, consts, x1):
    xrow = x.rearrange("b c h w -> (b c) (h w)")
    ximg = x.rearrange("b c h w -> (b c) h w")
    with ExitStack() as ctx:
        def sb(name, shape, dt=F32):
            return ctx.enter_context(nc.sbuf_tensor(name, shape, dt))

        def pb(name):
            return ctx.enter_context(nc.psum_tensor(name, [128, BANK], F32))

        def sem(name):
            return ctx.enter_context(nc.semaphore(name))

        ident = sb("ident1", [128, 128])
        w1 = sb("w1", [C, FF])
        w2 = sb("w2", [128, FT, C])
        b1 = sb("b1", [128, FT])
        b2 = sb("b2", [C, 1])
        gain = sb("gain", [C, 1])
        shift = sb("shift", [C, 1])
        scale_col = sb("scale_col", [C, 1])
        scale_row = sb("scale_row", [128, C])
        bias_row = sb("bias_row", [TOK, C])
        xpad = [sb(f"xpad{i}", [C, H + 2 * PAD1, COLS1]) for i in range(2)]
        win = sb("win", [WIN1, C, GI, NWIN1])
        taps = [sb(f"taps1_{i}", [WIN1, CQ, KT1, TOK]) for i in range(SLOTS1)]
        conv = sb("conv1", [TOK, BLOCKS, C])
        sq = sb("sq", [TOK, BLOCKS // GI, C])
        ln_sum = sb("ln_sum", [TOK, BLOCKS // GI])
        ln_mean = sb("ln_mean", [TOK, BLOCKS // GI])
        ln_ss = sb("ln_ss", [TOK, BLOCKS // GI])
        ln_var = sb("ln_var", [TOK, BLOCKS // GI])
        ln_rstd = sb("ln_rstd", [TOK, BLOCKS // GI])
        minus_half = sb("minus_half", [TOK, BLOCKS // GI])
        hn = [sb(f"hn{i}", [C, BT]) for i in range(2)]
        act_h = [sb(f"act_h{i}", [128, FT, BT]) for i in range(2)]
        xres = [sb(f"xres{i}", [C, BT]) for i in range(2)]
        x1o = [sb(f"x1o{i}", [C, BT]) for i in range(2)]

        ps_stage = [pb(f"ps_stage{i}") for i in range(2)]
        ps_back = [pb(f"ps_back{i}") for i in range(2)]
        ps_up = [pb(f"ps_up{i}") for i in range(FT)]
        ps_down = pb("ps_down")

        consts_in = sem("consts_in")
        prepared = sem("prepared")
        xpad_ready = [sem(f"xpad_ready{i}") for i in range(2)]
        taps_ready = [sem(f"taps1_ready{i}") for i in range(SLOTS1)]
        xres_ready = [sem(f"xres_ready{i}") for i in range(2)]
        x1_stored = [sem(f"x1_stored{i}") for i in range(2)]
        win_turned = sem("win_turned")
        win_kept_dve = sem("win_kept_dve")
        win_kept_act = sem("win_kept_act")
        conv_done = sem("conv_done")
        conv_kept = sem("conv_kept")
        ln_step = sem("ln_step")
        sq_ready = sem("sq_ready")
        rstd_ready = sem("rstd_ready")
        back_done = sem("back_done")
        hn_ready = sem("hn_ready")
        up_done = sem("up_done")
        gelu_done = sem("gelu_done")
        down_done = sem("down_done")
        x1_done = sem("x1_done")
        block = ctx.enter_context(nc.Block())

        LN = 6
        TURNS = GI * TURNS1
        TURN = {BANDS * (i - 1) + 3 + k: i * TURNS1 + 2 * k for i in range(1, GI) for k in range(TURNS1 // 2)}

        PREPARED = 4
        last = groups - 1

        @block.sync
        def _(sp):
            c = consts
            loads = [(ident[:, :], c["ident"]), (w1[:, :], c["w1"]),
                     (w2[:, :, :], c["w2"].rearrange("(t p) c -> p t c", p=128)),
                     (b1[:, :], c["b1"]),
                     (b2[:, :], c["b2"].rearrange("(p o) -> p o", o=1)),
                     (gain[:, :], c["ln_g"].rearrange("(p o) -> p o", o=1)),
                     (shift[:, :], c["ln_b"].rearrange("(p o) -> p o", o=1)),
                     (scale_col[:, :], c["ls"].rearrange("(p o) -> p o", o=1)),
                     (scale_row[:, :], c["ls"].partition_broadcast(128)),
                     (bias_row[:, :], c["cb1"].partition_broadcast(TOK))]
            for dst, src in loads:
                sp.dma_start(dst, src).then_inc(consts_in, 16)

            def load_image(f, i):
                sp.dma_start(xpad[i % 2][:, PAD1:PAD1 + H, PAD1:PAD1 + W],
                             ximg[ds((f * GI + i) * C, C), :, :]).then_inc(xpad_ready[i % 2], 16)

            def load_taps(q):
                slot = q % SLOTS1
                sp.dma_start(taps[slot][:, :, :, :], t1[q]).then_inc(taps_ready[slot], 16)

            def load_xres(f, u):
                sp.dma_start(xres[u % 2][:, :],
                             xrow[ds((f * GI + u // BANDS) * C, C), (u % BANDS) * BT:(u % BANDS + 1) * BT]
                             ).then_inc(xres_ready[u % 2], 16)

            sp.wait_ge(prepared, PREPARED)
            load_image(0, 0)
            load_image(0, 1)
            for q in range(SLOTS1):
                load_taps(q)
            load_xres(0, 0)
            load_xres(0, 1)
            for i in range(2, GI):
                sp.wait_ge(win_turned, TURNS1 * (i - 1))
                load_image(0, i)

            def group(g, more):
                if more:
                    sp.wait_ge(win_turned, (g + 1) * TURNS)
                    load_image(g + 1, 0)
                    load_image(g + 1, 1)
                for q in range(QUNITS):
                    if more or q + SLOTS1 < QUNITS:
                        sp.wait_ge(conv_done, g * QUNITS + q + 1)
                        load_taps((q + SLOTS1) % QUNITS)
                for u in range(UNITS):
                    if more and u in (BANDS, 2 * BANDS):
                        i = u // BANDS + 1
                        sp.wait_ge(win_turned, (g + 1) * TURNS + TURNS1 * (i - 1))
                        load_image(g + 1, i)
                    sp.wait_ge(x1_done, g * UNITS + u + 1)
                    sp.dma_start(x1[ds((g * GI + u // BANDS) * C, C), (u % BANDS) * BT:(u % BANDS + 1) * BT],
                                 x1o[u % 2][:, :]).then_inc(x1_stored[u % 2], 16)
                    if u + 2 < UNITS:
                        load_xres(g, u + 2)
                    elif more:
                        load_xres(g + 1, u + 2 - UNITS)

            if last:
                with sp.Fori(0, last) as g:
                    group(g, True)
            group(last, False)
            for p in range(2):
                sp.wait_ge(x1_stored[p], 16 * (groups * UNITS // 2 + 1))

        @block.gpsimd
        def _(pool):
            nc.gpsimd.memset(minus_half[:, :], -0.5).then_inc(prepared, 1)
            pool.sem_inc(x1_stored[0], 16)
            pool.sem_inc(x1_stored[1], 16)
            pool.wait_ge(prepared, PREPARED)

            def group(g):
                for i in range(GI):
                    pool.wait_ge(ln_step, (g * GI + i) * LN + 5)
                    nc.gpsimd.tensor_tensor(ln_rstd[:, :], ln_var[:, :], minus_half[:, :],
                                            ALU.pow).then_inc(rstd_ready, 1)

            with pool.Fori(0, groups) as g:
                group(g)

        @block.vector
        def _(dve):
            for p in range(2):
                nc.vector.memset(xpad[p][:, :, :], 0.0).then_inc(prepared, 1)
            dve.wait_ge(consts_in, 16 * 10)
            nc.vector.tensor_tensor(w2[:, :, :], w2[:, :, :],
                                    scale_row[:, :].unsqueeze(1).broadcast_to([128, FT, C]),
                                    ALU.mult)
            nc.vector.tensor_tensor(b2[:, :], b2[:, :], scale_col[:, :], ALU.mult).then_inc(prepared, 1)

            def keep_windows(f, n):
                dve.wait_ge(win_turned, f * TURNS + n + 1)
                nc.vector.tensor_copy(*window_copy(win, ps_stage, n)).then_inc(win_kept_dve, 1)

            def ln(g, i, step):
                base = (g * GI + i) * LN
                x_i = conv[:, i * IMG_BLK:(i + 1) * IMG_BLK, :]
                wide = [TOK, IMG_BLK, C]
                if step == 0:
                    nc.vector.tensor_reduce(ln_sum[:, :], x_i, AX_X, ALU.add).then_inc(ln_step, 1)
                elif step == 1:
                    dve.wait_ge(ln_step, base + 1)
                    nc.vector.tensor_scalar(ln_mean[:, :], ln_sum[:, :], 1.0 / C, None, ALU.mult).then_inc(ln_step, 1)
                elif step == 2:
                    dve.wait_ge(ln_step, base + 2)
                    nc.vector.tensor_tensor(x_i, x_i, ln_mean[:, :].unsqueeze(2).broadcast_to(wide),
                                            ALU.subtract).then_inc(ln_step, 1)
                elif step == 3:
                    dve.wait_ge(sq_ready, g * GI + i + 1)
                    nc.vector.tensor_reduce(ln_ss[:, :], sq[:, :, :], AX_X, ALU.add).then_inc(ln_step, 1)
                elif step == 4:
                    dve.wait_ge(ln_step, base + 4)
                    nc.vector.tensor_scalar(ln_var[:, :], ln_ss[:, :], 1.0 / C, LN_EPS, ALU.mult,
                                            ALU.add).then_inc(ln_step, 1)
                else:
                    dve.wait_ge(rstd_ready, g * GI + i + 1)
                    nc.vector.tensor_tensor(x_i, x_i, ln_rstd[:, :].unsqueeze(2).broadcast_to(wide),
                                            ALU.mult).then_inc(ln_step, 1)

            def normed(g, u):
                dve.wait_ge(back_done, g * UNITS + u + 1)
                nc.vector.tensor_scalar(hn[u % 2][:, :], ps_back[u % 2][0:C, 0:BT], gain[:, 0:1], shift[:, 0:1],
                                        ALU.mult, ALU.add).then_inc(hn_ready, 1)

            def residual(g, u):
                dve.wait_ge(down_done, g * UNITS + u + 1)
                dve.wait_ge(xres_ready[u % 2], (g * (UNITS // 2) + u // 2 + 1) * 16)
                dve.wait_ge(x1_stored[u % 2], (g * (UNITS // 2) + u // 2 + 1) * 16)
                nc.vector.scalar_tensor_tensor(x1o[u % 2][:, :], ps_down[0:C, 0:BT], b2[:, 0:1],
                                               xres[u % 2][:, :], ALU.add, ALU.add).then_inc(x1_done, 1)

            def group(g, more):
                for q in range(QUNITS):
                    dve.wait_ge(conv_done, g * QUNITS + q + 1)
                    nc.vector.tensor_tensor(
                        conv[:, :, q * CQ:(q + 1) * CQ].rearrange("p b c -> p c b"),
                        ps_stage[q % 2][0:TOK, 0:CQ * BLOCKS].rearrange("p (c b) -> p c b", c=CQ),
                        bias_row[:, q * CQ:(q + 1) * CQ].unsqueeze(2).broadcast_to([TOK, CQ, BLOCKS]),
                        ALU.add).then_inc(conv_kept, 1)
                dve.wait_ge(conv_kept, g * QUNITS + QUNITS)
                for step in range(LN):
                    ln(g, 0, step)
                    if more:
                        for n in {0: [0], 2: [2], 3: [4], 4: [6]}.get(step, []):
                            keep_windows(g + 1, n)
                normed(g, 0)
                for u in range(UNITS):
                    if u + 1 < UNITS:
                        normed(g, u + 1)
                    if more and u in TURN:
                        keep_windows(g + 1, TURN[u])
                    if u > 0:
                        residual(g, u - 1)
                    i, k = u // BANDS + 1, u % BANDS
                    if i < GI:
                        for step in {1: [0], 2: [1, 2], 4: [3, 4], 5: [5]}.get(k, []):
                            ln(g, i, step)
                residual(g, UNITS - 1)

            for n in range(0, TURNS, 2):
                keep_windows(0, n)
            if last:
                with dve.Fori(0, last) as g:
                    group(g, True)
            group(last, False)

        @block.scalar
        def _(act):
            def keep_windows(f, n):
                act.wait_ge(win_turned, f * TURNS + n + 1)
                nc.scalar.activation(*window_copy(win, ps_stage, n), ACT.Copy).then_inc(win_kept_act, 1)

            def square(g, i):
                act.wait_ge(ln_step, (g * GI + i) * LN + 3)
                nc.scalar.activation(sq[:, :, :], conv[:, i * IMG_BLK:(i + 1) * IMG_BLK, :],
                                     ACT.Square).then_inc(sq_ready, 1)

            def gelu(g, u):
                if u >= 2:
                    act.wait_ge(down_done, g * UNITS + u - 1)
                for t in range(FT):
                    act.wait_ge(up_done, (g * UNITS + u) * FT + t + 1)
                    nc.scalar.activation(act_h[u % 2][:, t, :], ps_up[t][:, 0:BT], ACT.Gelu,
                                         bias=b1[:, t:t + 1]).then_inc(gelu_done, 1)

            def group(g, more):
                if more:
                    keep_windows(g + 1, 1)
                square(g, 0)
                if more:
                    for n in (3, 5, 7):
                        keep_windows(g + 1, n)
                for u in range(UNITS):
                    gelu(g, u)
                    if more and u in TURN:
                        keep_windows(g + 1, TURN[u] + 1)
                    if u % BANDS == 3 and u // BANDS + 1 < GI:
                        square(g, u // BANDS + 1)

            act.wait_ge(consts_in, 16 * 10)
            for n in range(1, TURNS, 2):
                keep_windows(0, n)
            if last:
                with act.Fori(0, last) as g:
                    group(g, True)
            group(last, False)

        @block.tensor
        def _(pe):
            def turn_windows(f, first, n):
                i, part = n // TURNS1, n % TURNS1
                if part == 0:
                    pe.wait_ge(xpad_ready[i % 2], (f * (GI // 2) + i // 2 + 1) * 16)
                if n >= 2:
                    pe.wait_ge((win_kept_dve, win_kept_act)[n % 2], f * (TURNS // 2) + n // 2)
                elif not first:
                    pe.wait_ge(conv_kept, f * QUNITS)
                pixels = xpad[i % 2][:, :, :].rearrange("p r w -> p (r w)")
                for j, w in enumerate(range(part * TW, min((part + 1) * TW, NWIN1))):
                    mm = nc.tensor.transpose(ps_stage[n % 2][0:WIN1, j * C:(j + 1) * C],
                                             pixels[:, w * WIN1:(w + 1) * WIN1], ident[0:C, 0:C])
                mm.then_inc(win_turned, 1)

            def convolve(g):
                pe.wait_ge(win_kept_dve, (g + 1) * (TURNS // 2))
                pe.wait_ge(win_kept_act, (g + 1) * (TURNS // 2))
                for q in range(QUNITS):
                    pe.wait_ge(taps_ready[q % SLOTS1], (g * (QUNITS // SLOTS1) + q // SLOTS1 + 1) * 16)
                    if q >= 2:
                        pe.wait_ge(conv_kept, g * QUNITS + q - 1)
                    for c in range(CQ):
                        for k in range(KT1):
                            mm = nc.tensor.matmul(
                                ps_stage[q % 2][0:TOK, c * BLOCKS:(c + 1) * BLOCKS],
                                taps[q % SLOTS1][:, c, k, :],
                                win[:, q * CQ + c, :, k:k + IMG_BLK],
                                start=(k == 0), stop=(k == KT1 - 1))
                    mm.then_inc(conv_done, 1)

            def back(g, u):
                if u % BANDS == 0:
                    pe.wait_ge(ln_step, (g * GI + u // BANDS) * LN + LN)
                if u >= 2:
                    pe.wait_ge(hn_ready, g * UNITS + u - 1)
                for j in range(BLKS):
                    mm = nc.tensor.transpose(ps_back[u % 2][0:C, j * TOK:(j + 1) * TOK],
                                             conv[:, u * BLKS + j, :], ident[0:TOK, 0:TOK])
                mm.then_inc(back_done, 1)

            def up(g, u):
                pe.wait_ge(hn_ready, g * UNITS + u + 1)
                for t in range(FT):
                    if u > 0:
                        pe.wait_ge(gelu_done, (g * UNITS + u - 1) * FT + t + 1)
                    nc.tensor.matmul(ps_up[t][:, 0:BT], w1[:, t * 128:(t + 1) * 128], hn[u % 2][:, :],
                                     start=True, stop=True).then_inc(up_done, 1)

            def down(g, u):
                pe.wait_ge(gelu_done, (g * UNITS + u + 1) * FT)
                if u > 0:
                    pe.wait_ge(x1_done, g * UNITS + u)
                for t in range(FT):
                    mm = nc.tensor.matmul(ps_down[0:C, 0:BT], w2[:, t, :], act_h[u % 2][:, t, :],
                                          start=(t == 0), stop=(t == FT - 1))
                mm.then_inc(down_done, 1)

            def group(g, more):
                convolve(g)
                if more:
                    for n in range(TURNS1):
                        turn_windows(g + 1, False, n)
                back(g, 0)
                for u in range(UNITS):
                    up(g, u)
                    if u + 1 < UNITS:
                        back(g, u + 1)
                    if more and u in TURN:
                        turn_windows(g + 1, False, TURN[u])
                        turn_windows(g + 1, False, TURN[u] + 1)
                    if u > 0:
                        down(g, u - 1)
                down(g, UNITS - 1)

            pe.wait_ge(consts_in, 16 * 10)
            pe.wait_ge(prepared, PREPARED)
            for n in range(TURNS):
                turn_windows(0, True, n)
            if last:
                with pe.Fori(0, last) as g:
                    group(g, True)
            group(last, False)


def layer1(nc, groups, x1, t2, consts, out):
    x1img = x1.rearrange("r (h w) -> r h w", h=H)
    with ExitStack() as ctx:
        def sb(name, shape, dt=F32):
            return ctx.enter_context(nc.sbuf_tensor(name, shape, dt))

        def pb(name):
            return ctx.enter_context(nc.psum_tensor(name, [128, BANK], F32))

        def sem(name):
            return ctx.enter_context(nc.semaphore(name))

        ident = sb("ident2", [128, 128])
        xproj = sb("xproj", [128, TILES, XD])
        dtw = sb("dtw", [XD, TILES, 128])
        sel = sb("sel", [3 * BC, 2, TILES, N, 128], BF16)
        skip = sb("skip", [128, TILES, 128])
        ds_col = sb("ds_col", [128, TILES])
        dt_bias = sb("dt_bias", [128, TILES])
        conv_bias = sb("conv_bias", [128, TILES])
        a_neg = sb("a_neg", [128, TILES, N])
        zeros = sb("zeros", [128, BT])
        q_first = sb("q_first", [128, STEPS])
        xpad = sb("x1pad", [C, H + 2 * PAD2, COLS2])
        win = sb("win2", [WIN2, CB, GI, NWIN2])
        taps = [sb(f"taps2_{i}", [WIN2, CQ, KT2, TOK]) for i in range(SLOTS2)]
        conv = sb("conv2", [TOK, IMG_BLK, GI * C])
        xs = sb("xs", [128, TILES, L])
        xd = sb("xd", [XD, BT])
        rest = sb("rest", [3 * BC, BT])
        coarse = sb("coarse", [3 * BC, BT], BF16)
        masks = sb("masks", [3 * BC, 2])
        parts = [sb(f"parts{i}", [3 * BC, BT], BF16) for i in range(2)]
        z_pos = sb("z_pos", [128, TILES, BT])
        z_log = sb("z_log", [128, TILES, BT])
        delta = sb("delta", [128, TILES, BT])
        dxs = sb("dxs", [128, TILES, BT])
        d_a = [sb(f"d_a{i}", [128, BT]) for i in range(2)]
        q = [sb(f"q{i}", [128, BT]) for i in range(2)]
        u = [sb(f"u{i}", [128, BT]) for i in range(2)]
        h = [sb(f"h{i}", [128, BT]) for i in range(2)]
        hc = [sb(f"hc{i}", [128, BT]) for i in range(2)]
        q_last = sb("q_last", [128, STEPS])
        h_last = sb("h_last", [128, STEPS])
        y = [sb(f"y{i}", [128, BT]) for i in range(2)]

        ps_front = [pb(f"ps_front{i}") for i in range(2)]
        ps_prep = [pb(f"ps_prep{i}") for i in range(2)]
        ps_b = pb("ps_b")
        ps_c = pb("ps_c")
        ps_y = [pb(f"ps_y{i}") for i in range(2)]

        consts_in = sem("consts2_in")
        a_logs_in = sem("a_logs_in")
        prepared = sem("prepared2")
        slab_ready = [sem(f"slab_ready{i}") for i in range(SLABS)]
        taps_ready = [sem(f"taps2_ready{i}") for i in range(SLOTS2)]
        front_done = sem("front_done")
        front_kept = sem("front_kept")
        prep_done = sem("prep_done")
        prep_kept = sem("prep_kept")
        xd_ready = sem("xd_ready")
        split_step = sem("split_step")
        z_step = sem("z_step")
        delta_ready = sem("delta_ready")
        dxs_ready = sem("dxs_ready")
        d_a_ready = sem("d_a_ready")
        b_ready = sem("b_ready")
        c_ready = sem("c_ready")
        clamp_done = sem("clamp_done")
        q_done = sem("q_done")
        u_done = sem("u_done")
        gated = sem("gated")
        h_done = sem("h_done")
        hc_done = sem("hc_done")
        q_kept = sem("q_kept")
        h_kept = sem("h_kept")
        y_done = sem("y_done")
        y_kept = sem("y_kept")
        y_stored = [sem(f"y_stored{i}") for i in range(2)]
        block = ctx.enter_context(nc.Block())

        last = groups - 1
        CONSTS = 16 * 8
        PREPARED = 6
        S = BANDS * STEPS
        RUNS = BANDS * TILES
        PREPS = RUNS + BANDS * (1 + TILES)
        SPLIT = 6
        KEPT = S + STEPS
        FRONT = CBS * (GI * TURNS2 + CB // CQ)
        units = []
        for cb in range(CBS):
            units += [("turn", cb, i, p) for i in range(GI) for p in range(TURNS2)]
            units += [("conv", cb, cu, 0) for cu in range(CB // CQ)]
        at_step = {i * (S - 4) // FRONT: i for i in range(FRONT)}
        step_of = {i: s for s, i in at_step.items()}
        turn_unit = [units.index(("turn", k // GI, k % GI, TURNS2 - 1)) for k in range(CBS * GI)]
        conv_unit = [units.index(("conv", k // (CB // CQ), k % (CB // CQ), 0)) for k in range(QUNITS)]

        @block.sync
        def _(sp):
            for dst, src in [(ident[:, :], consts["ident"]), (xproj[:, :, :], consts["xproj"]),
                             (dtw[3 * BC:XD, :, :], consts["dtw"]), (sel[:, :, :, :, :], consts["sel"]),
                             (ds_col[:, :], consts["ds"]), (dt_bias[:, :], consts["dt_bias"]),
                             (conv_bias[:, :], consts["cb2"]), (masks[:, :], consts["masks"])]:
                sp.dma_start(dst, src).then_inc(consts_in, 16)
            sp.dma_start(a_neg[:, :, :], consts["a_logs"]).then_inc(a_logs_in, 16)

            def load_slab(f, first, k):
                if k >= SLABS:
                    sp.wait_ge(front_done, f * FRONT + turn_unit[k - SLABS] + 1)
                elif not first:
                    sp.wait_ge(front_done, (f - 1) * FRONT + turn_unit[k - SLABS] + 1)
                rows = slice(CB * (k % SLABS), CB * (k % SLABS) + CB)
                sp.dma_start(xpad[rows, PAD2:PAD2 + H, PAD2:PAD2 + W],
                             x1img[ds((f * GI + k % GI) * C + CB * (k // GI), CB), :, :]
                             ).then_inc(slab_ready[k % SLABS], 16)

            def load_taps(f, first, k):
                if k >= SLOTS2:
                    sp.wait_ge(front_done, f * FRONT + conv_unit[k - SLOTS2] + 1)
                elif not first:
                    sp.wait_ge(front_done, (f - 1) * FRONT + conv_unit[k - SLOTS2] + 1)
                sp.dma_start(taps[k % SLOTS2][:, :, :, :], t2[k]).then_inc(taps_ready[k % SLOTS2], 16)

            loads = []
            for cb in range(CBS):
                loads += [(load_slab, GI * cb + i, turn_unit[GI * cb + i]) for i in range(GI)]
                loads += [(load_taps, k, conv_unit[k]) for k in range(cb * CB // CQ, (cb + 1) * CB // CQ)]

            sp.wait_ge(prepared, PREPARED)
            for load, k, _ in loads:
                load(0, True, k)

            def store(g, r):
                b, t = r // TILES, r % TILES
                sp.wait_ge(y_kept, g * RUNS + r + 1)
                sp.dma_start(out[ds(g * GI * C + t * 128, 128), b * BT:(b + 1) * BT],
                             y[r % 2][:, :]).then_inc(y_stored[r % 2], 16)

            def group(g, more):
                todo = list(loads) if more else []
                for s in range(S):
                    while todo and step_of[todo[0][2]] <= s + AHEAD:
                        load, k, _ = todo.pop(0)
                        load(g + 1, False, k)
                    if s >= N + 2 and (s - N - 2) % N == 0:
                        store(g, (s - N - 2) // N)
                store(g, RUNS - 1)

            if last:
                with sp.Fori(0, last) as g:
                    group(g, True)
            group(last, False)
            for p in range(2):
                sp.wait_ge(y_stored[p], (groups * ((RUNS + 1 - p) // 2) + 1) * 16)

        @block.gpsimd
        def _(pool):
            nc.gpsimd.memset(xpad[:, :, :], 0.0).then_inc(prepared, 1)
            nc.gpsimd.memset(zeros[:, :], 0.0).then_inc(prepared, 1)
            nc.gpsimd.memset(q_first[:, :], float(np.float32(1) / np.float32(EPS))).then_inc(prepared, 1)
            pool.sem_inc(y_stored[0], 16)
            pool.sem_inc(y_stored[1], 16)
            pool.wait_ge(prepared, PREPARED)
            pool.wait_ge(consts_in, CONSTS)

            def add(o, a, b):
                return nc.gpsimd.tensor_tensor(o, a, b, ALU.add)

            def first_states():
                add(q_last[:, :], q_first[:, :], zeros[:, 0:STEPS]).then_inc(q_kept, STEPS)
                add(h_last[:, :], zeros[:, 0:STEPS], zeros[:, 0:STEPS]).then_inc(h_kept, STEPS)

            def split(g, b, k):
                v = xd[0:3 * BC, :]
                p = parts[b % 2]
                if k == 0:
                    pool.wait_ge(xd_ready, g * BANDS + b + 1)
                    ins = add(coarse[:, :], v, zeros[0:3 * BC, :])
                else:
                    pool.wait_ge(split_step, (g * BANDS + b) * SPLIT + k)
                    mask = masks[:, k // 3:k // 3 + 1].broadcast_to([3 * BC, BT])
                    if k in (1, 4):
                        ins = nc.gpsimd.tensor_tensor(coarse[:, :], coarse[:, :], mask, ALU.mult)
                    elif k == 2:
                        ins = nc.gpsimd.tensor_tensor(rest[:, :], v, coarse[:, :], ALU.subtract)
                    elif k == 3:
                        ins = add(coarse[:, :], rest[:, :], zeros[0:3 * BC, :])
                    else:
                        ins = nc.gpsimd.tensor_tensor(p[:, :], rest[:, :], coarse[:, :], ALU.subtract)
                ins.then_inc(split_step, 1)

            def sum_delta(g, b, t):
                pool.wait_ge(z_step, (g * RUNS + b * TILES + t) * ZSTEPS + ZSTEPS)
                if b > 0:
                    pool.wait_ge(d_a_ready, g * S + (b - 1) * STEPS + (t + 1) * N)
                    pool.wait_ge(u_done, g * S + (b - 1) * STEPS + (t + 1) * N)
                add(delta[:, t, :], z_pos[:, t, :], z_log[:, t, :]).then_inc(delta_ready, 1)

            def times_x(g, b, t):
                pool.wait_ge(delta_ready, g * RUNS + b * TILES + t + 1)
                nc.gpsimd.tensor_tensor(dxs[:, t, :], delta[:, t, :], xs[:, t, b * BT:(b + 1) * BT],
                                        ALU.mult).then_inc(dxs_ready, 1)

            def group(g, more):
                for k in range(SPLIT):
                    split(g, 0, k)
                for t in range(TILES):
                    sum_delta(g, 0, t)
                    times_x(g, 0, t)
                for b in range(BANDS):
                    for j in range(STEPS):
                        s = b * STEPS + j
                        pool.wait_ge(q_done, g * S + s + 1)
                        add(q_last[:, j:j + 1], q[s % 2][:, BT - 1:BT], zeros[:, 0:1]).then_inc(q_kept, 1)
                        if b + 1 < BANDS:
                            if 1 <= j <= SPLIT:
                                split(g, b + 1, j - 1)
                            elif j in (7, 9):
                                sum_delta(g, b + 1, (j - 7) // 2)
                            elif j in (8, 10):
                                times_x(g, b + 1, (j - 8) // 2)
                        pool.wait_ge(h_done, g * S + s + 1)
                        add(h_last[:, j:j + 1], h[s % 2][:, BT - 1:BT], zeros[:, 0:1]).then_inc(h_kept, 1)
                    if b + 1 < BANDS:
                        sum_delta(g, b + 1, TILES - 1)
                        times_x(g, b + 1, TILES - 1)
                if more:
                    pool.wait_ge(q_kept, (g + 1) * KEPT)
                    pool.wait_ge(h_kept, (g + 1) * KEPT)
                    first_states()

            first_states()
            if last:
                with pool.Fori(0, last) as g:
                    group(g, True)
            group(last, False)

        @block.vector
        def _(dve):
            dve.wait_ge(consts_in, CONSTS)
            for t in range(TILES):
                ins = nc.vector.tensor_scalar(skip[:, t, :], ident[:, :], ds_col[:, t:t + 1], None, ALU.mult)
            ins.then_inc(prepared, 1)
            dve.wait_ge(prepared, PREPARED - 1)
            nc.vector.tensor_scalar(a_neg[:, :, :], a_neg[:, :, :], -1.0, None, ALU.mult).then_inc(prepared, 1)

            def clamp(n, j):
                dve.wait_ge(d_a_ready, n + j + 1)
                nc.vector.tensor_scalar(d_a[j % 2][:, :], d_a[j % 2][:, :], float(np.float32(EPS)), None,
                                        ALU.max).then_inc(clamp_done, 1)

            def times_b(n, runs, j):
                dve.wait_ge(b_ready, n + j + 1)
                if j % N == 0:
                    dve.wait_ge(dxs_ready, runs + j // N + 1)
                nc.vector.tensor_tensor(u[j % 2][:, :], dxs[:, j // N, :], ps_b[:, 0:BT], ALU.mult).then_inc(u_done, 1)

            def scan_q(n, kept, j):
                dve.wait_ge(clamp_done, n + j + 1)
                dve.wait_ge(q_kept, kept + j)
                nc.vector.tensor_tensor_scan(q[j % 2][:, :], d_a[j % 2][:, :], zeros[:, :], q_last[:, j:j + 1],
                                             ALU.mult, ALU.add).then_inc(q_done, 1)

            def gate(n, j):
                dve.wait_ge(q_done, n + j + 1)
                dve.wait_ge(u_done, n + j + 1)
                nc.vector.scalar_tensor_tensor(u[j % 2][:, :], q[j % 2][:, :], 1.0, u[j % 2][:, :],
                                               ALU.min, ALU.mult).then_inc(gated, 1)

            def scan_h(n, kept, j):
                dve.wait_ge(gated, n + j + 1)
                dve.wait_ge(h_kept, kept + j)
                nc.vector.tensor_tensor_scan(h[j % 2][:, :], d_a[j % 2][:, :], u[j % 2][:, :], h_last[:, j:j + 1],
                                             ALU.mult, ALU.add).then_inc(h_done, 1)

            def times_c(n, j):
                dve.wait_ge(h_done, n + j + 1)
                dve.wait_ge(c_ready, n + j + 1)
                nc.vector.tensor_tensor(hc[j % 2][:, :], h[j % 2][:, :], ps_c[:, 0:BT], ALU.mult).then_inc(hc_done, 1)

            with dve.Fori(0, groups) as g:
                with dve.Fori(0, BANDS) as b:
                    n = g * S + b * STEPS
                    runs = g * RUNS + b * TILES
                    kept = g * KEPT + b * STEPS + STEPS - 1
                    clamp(n, 0)
                    times_b(n, runs, 0)
                    for j in range(STEPS):
                        scan_q(n, kept, j)
                        if j > 0:
                            times_c(n, j - 1)
                        gate(n, j)
                        if j + 1 < STEPS:
                            clamp(n, j + 1)
                        scan_h(n, kept, j)
                        if j + 1 < STEPS:
                            times_b(n, runs, j + 1)
                    times_c(n, STEPS - 1)

        @block.scalar
        def _(act):
            def keep_front(f, i):
                kind, cb, k, p = units[i]
                act.wait_ge(front_done, f * FRONT + i + 1)
                if kind == "turn":
                    src = ps_front[i % 2][0:WIN2, 0:TW2 * CB].rearrange("p (w c) -> p w c", c=CB)
                    dst = win[:, :, k, p * TW2:(p + 1) * TW2].rearrange("p c w -> p w c")
                else:
                    c0 = cb * CB + k * CQ
                    src = ps_front[i % 2][0:TOK, 0:CQ * BLOCKS].rearrange("p (c i b) -> p c i b", c=CQ, i=GI)
                    dst = conv[:, :, :].rearrange("p b (i c) -> p c i b", i=GI)[:, c0:c0 + CQ, :, :]
                nc.scalar.activation(dst, src, ACT.Copy).then_inc(front_kept, 1)

            def silu(g, r):
                b, t = r // TILES, r % TILES
                act.wait_ge(prep_done, g * PREPS + r + 1)
                nc.scalar.activation(xs[:, t, b * BT:(b + 1) * BT], ps_prep[r % 2][:, 0:BT], ACT.Silu,
                                     bias=conv_bias[:, t:t + 1]).then_inc(prep_kept, 1)

            def keep_xd(g, b):
                r = RUNS + b * (1 + TILES)
                act.wait_ge(prep_done, g * PREPS + r + 1)
                if b > 0:
                    act.wait_ge(split_step, (g * BANDS + b) * SPLIT)
                nc.scalar.activation(xd[:, :], ps_prep[r % 2][0:XD, 0:BT], ACT.Copy).then_inc(xd_ready, 1)

            def softplus(g, b, t, late):
                r = RUNS + b * (1 + TILES) + 1 + t
                n = (g * RUNS + b * TILES + t) * ZSTEPS
                bias = dt_bias[:, t:t + 1]
                if late:
                    act.wait_ge(z_step, n + 3)
                    nc.scalar.activation(z_log[:, t, :], z_log[:, t, :], ACT.Ln, bias=1.0).then_inc(z_step, 1)
                    return
                act.wait_ge(prep_done, g * PREPS + r + 1)
                if b > 0:
                    act.wait_ge(delta_ready, g * RUNS + (b - 1) * TILES + t + 1)
                src = ps_prep[r % 2][:, 0:BT]
                nc.scalar.activation(z_log[:, t, :], src, ACT.Abs, bias=bias).then_inc(z_step, 1)
                nc.scalar.activation(z_pos[:, t, :], src, ACT.Relu, bias=bias).then_inc(z_step, 1)
                act.wait_ge(z_step, n + 2)
                nc.scalar.activation(z_log[:, t, :], z_log[:, t, :], ACT.Exp, scale=-1.0).then_inc(z_step, 1)

            def exp_a(g, s):
                b, t, n = s // STEPS, s % STEPS // N, s % N
                if n == 0:
                    act.wait_ge(delta_ready, g * RUNS + b * TILES + t + 1)
                if s >= 2:
                    act.wait_ge(h_done, g * S + s - 1)
                nc.scalar.activation(d_a[s % 2][:, :], delta[:, t, :], ACT.Exp,
                                     scale=a_neg[:, t, n:n + 1]).then_inc(d_a_ready, 1)

            def keep_y(g, r):
                act.wait_ge(y_done, g * RUNS + r + 1)
                act.wait_ge(y_stored[r % 2], (g * ((RUNS + 1 - r % 2) // 2) + r // 2 + 1) * 16)
                nc.scalar.activation(y[r % 2][:, :], ps_y[r % 2][:, 0:BT], ACT.Copy).then_inc(y_kept, 1)

            def group(g, more):
                act.preload_act_table_set("silu_and_others")
                for r in range(RUNS):
                    silu(g, r)
                act.preload_act_table_set("natural_log_exp_and_others")
                keep_xd(g, 0)
                for t in range(TILES):
                    softplus(g, 0, t, False)
                    softplus(g, 0, t, True)
                exp_a(g, 0)
                for s in range(S):
                    b, j = s // STEPS, s % STEPS
                    if s + 1 < S:
                        exp_a(g, s + 1)
                    if more and s in at_step:
                        keep_front(g + 1, at_step[s])
                    if s >= N + 1 and (s - N - 1) % N == 0:
                        keep_y(g, (s - N - 1) // N)
                    if b + 1 < BANDS:
                        if j == 1:
                            keep_xd(g, b + 1)
                        if 4 <= j < 4 + TILES:
                            softplus(g, b + 1, j - 4, True)
                        if 3 <= j < 3 + TILES:
                            softplus(g, b + 1, j - 3, False)
                keep_y(g, RUNS - 1)

            act.wait_ge(a_logs_in, 16)
            act.preload_act_table_set("natural_log_exp_and_others")
            nc.scalar.activation(a_neg[:, :, :], a_neg[:, :, :], ACT.Exp).then_inc(prepared, 1)
            act.wait_ge(prepared, PREPARED)
            for i in range(FRONT):
                keep_front(0, i)
            if last:
                with act.Fori(0, last) as g:
                    group(g, True)
            group(last, False)

        @block.tensor
        def _(pe):
            def front_waits(f, i):
                kind, cb, k, p = units[i]
                if kind == "turn":
                    slab = cb * GI + k
                    pe.wait_ge(slab_ready[slab % SLABS], (f * (CBS * GI // SLABS) + slab // SLABS + 1) * 16)
                    if i >= 2:
                        pe.wait_ge(front_kept, f * FRONT + i - 1)
                else:
                    n = cb * (CB // CQ) + k
                    pe.wait_ge(taps_ready[n % SLOTS2], (f * (QUNITS // SLOTS2) + n // SLOTS2 + 1) * 16)
                    pe.wait_ge(front_kept, f * FRONT + (i if k == 0 else i - 1))

            def front(i):
                kind, cb, k, p = units[i]
                if kind == "turn":
                    slab = cb * GI + k
                    rows = slice(CB * (slab % SLABS), CB * (slab % SLABS) + CB)
                    pixels = xpad[rows, :, :].rearrange("p r w -> p (r w)")
                    for w in range(TW2):
                        mm = nc.tensor.transpose(ps_front[i % 2][0:WIN2, w * CB:(w + 1) * CB],
                                                 pixels[:, (p * TW2 + w) * WIN2:(p * TW2 + w + 1) * WIN2],
                                                 ident[rows, rows])
                else:
                    n = cb * (CB // CQ) + k
                    for c in range(CQ):
                        for w in range(KT2):
                            mm = nc.tensor.matmul(
                                ps_front[i % 2][0:TOK, c * BLOCKS:(c + 1) * BLOCKS],
                                taps[n % SLOTS2][:, c, w, :],
                                win[:, k * CQ + c, :, w:w + IMG_BLK],
                                start=(w == 0), stop=(w == KT2 - 1))
                mm.then_inc(front_done, 1)

            def prep_bank(g, r):
                b, kind = (r - 2 - RUNS) // (1 + TILES), (r - 2 - RUNS) % (1 + TILES)
                if 2 <= r < RUNS + 2:
                    pe.wait_ge(prep_kept, g * RUNS + r - 1)
                elif r >= RUNS + 2 and kind == 0:
                    pe.wait_ge(xd_ready, g * BANDS + b + 1)
                elif r >= RUNS + 2:
                    pe.wait_ge(z_step, (g * RUNS + b * TILES + kind - 1) * ZSTEPS + 2)
                return ps_prep[r % 2]

            def back(g, r):
                b, t = r // TILES, r % TILES
                bank = prep_bank(g, r)
                for j in range(BLKS):
                    mm = nc.tensor.transpose(bank[:, j * TOK:(j + 1) * TOK],
                                             conv[:, b * BLKS + j, t * 128:(t + 1) * 128], ident[0:TOK, 0:TOK])
                mm.then_inc(prep_done, 1)

            def project(g, b):
                if b == 0:
                    pe.wait_ge(prep_kept, (g + 1) * RUNS)
                bank = prep_bank(g, RUNS + b * (1 + TILES))
                for t in range(TILES):
                    mm = nc.tensor.matmul(bank[0:XD, 0:BT], xproj[:, t, :], xs[:, t, b * BT:(b + 1) * BT],
                                          start=(t == 0), stop=(t == TILES - 1))
                mm.then_inc(prep_done, 1)

            def delta_rows(g, b, t):
                bank = prep_bank(g, RUNS + b * (1 + TILES) + 1 + t)
                pe.wait_ge(xd_ready, g * BANDS + b + 1)
                nc.tensor.matmul(bank[:, 0:BT], dtw[3 * BC:XD, t, :], xd[3 * BC:XD, :],
                                 start=True, stop=True).then_inc(prep_done, 1)

            def spread_b(g, s):
                b, j = s // STEPS, s % STEPS
                if j == 0:
                    pe.wait_ge(split_step, (g * BANDS + b + 1) * SPLIT)
                if s > 0:
                    pe.wait_ge(u_done, g * S + s)
                nc.tensor.matmul(ps_b[:, 0:BT], sel[:, 0, j // N, j % N, :], parts[b % 2][:, :],
                                 start=True, stop=True).then_inc(b_ready, 1)

            def spread_c(g, s):
                b, j = s // STEPS, s % STEPS
                if s > 0:
                    pe.wait_ge(hc_done, g * S + s)
                nc.tensor.matmul(ps_c[:, 0:BT], sel[:, 1, j // N, j % N, :], parts[b % 2][:, :],
                                 start=True, stop=True).then_inc(c_ready, 1)

            def add_y(g, s):
                b, t, n = s // STEPS, s % STEPS // N, s % N
                r = b * TILES + t
                if n == 0 and r >= 2:
                    pe.wait_ge(y_kept, g * RUNS + r - 1)
                pe.wait_ge(hc_done, g * S + s + 1)
                nc.tensor.matmul(ps_y[r % 2][:, 0:BT], ident[:, :], hc[s % 2][:, :], start=(n == 0), stop=False)
                if n == N - 1:
                    nc.tensor.matmul(ps_y[r % 2][:, 0:BT], skip[:, t, :], xs[:, t, b * BT:(b + 1) * BT],
                                     start=False, stop=True).then_inc(y_done, 1)

            def group(g, more):
                pe.wait_ge(front_kept, (g + 1) * FRONT)
                for r in range(RUNS):
                    back(g, r)
                project(g, 0)
                for t in range(TILES):
                    delta_rows(g, 0, t)
                spread_b(g, 0)
                for s in range(S):
                    b, j = s // STEPS, s % STEPS
                    if s + 1 < S:
                        spread_b(g, s + 1)
                    if more and s in at_step:
                        front_waits(g + 1, at_step[s])
                    spread_c(g, s)
                    if more and s in at_step:
                        front(at_step[s])
                    if s > 0:
                        add_y(g, s - 1)
                    if b + 1 < BANDS:
                        if j == 0:
                            project(g, b + 1)
                        if 2 <= j < 2 + TILES:
                            delta_rows(g, b + 1, j - 2)
                add_y(g, S - 1)

            pe.wait_ge(consts_in, CONSTS)
            pe.wait_ge(prepared, PREPARED)
            for i in range(FRONT):
                front_waits(0, i)
                front(i)
            if last:
                with pe.Fori(0, last) as g:
                    group(g, True)
            group(last, False)


def banded(w, k):
    cols = W + k - 1
    kt = (ROWS + k - 1) // ROWS
    t = np.zeros((C, kt * ROWS, cols, ROWS, W), np.float32)
    for o in range(ROWS):
        for j in range(W):
            t[:, o:o + k, j:j + k, o, j] = w
    t = t.reshape(QUNITS, CQ, kt, ROWS * cols, TOK).transpose(0, 3, 1, 2, 4)
    return np.ascontiguousarray(t)


def lay_out(i):
    def rows(a):
        a = np.tile(a, (GI,) + (1,) * (a.ndim - 1))
        return np.ascontiguousarray(a.reshape((TILES, 128) + a.shape[1:]).swapaxes(0, 1))

    image, channel = np.divmod(np.arange(TILES * 128).reshape(TILES, 128), C)
    xproj = np.zeros((128, TILES, XD), np.float32)
    dtw = np.zeros((GI * R, TILES, 128), np.float32)
    sel = np.zeros((3 * BC, 2, TILES, N, 128), mybir.dt.np(BF16))
    for t in range(TILES):
        for p in range(128):
            m, c = image[t, p], channel[t, p]
            for part in range(3):
                at = part * BC + m * N
                xproj[p, t, at:at + N] = i["L1_conv_x_proj_w"][R:R + N, c]
                xproj[p, t, at + GI * N:at + GI * N + N] = i["L1_conv_x_proj_w"][R + N:, c]
                for n in range(N):
                    sel[at + n, 0, t, n, p] = 1
                    sel[at + GI * N + n, 1, t, n, p] = 1
            xproj[p, t, 3 * BC + m * R:3 * BC + (m + 1) * R] = i["L1_conv_x_proj_w"][:R, c]
            dtw[m * R:(m + 1) * R, t, p] = i["L1_conv_dt_w"][c]
    return {
        "x": i["x"], "t1": banded(i["L0_conv_conv_w"][:, 0], K1), "ident": np.eye(128, dtype=np.float32),
        "w1": i["L0_conv_w1"], "w2": i["L0_conv_w2"], "b1": np.ascontiguousarray(i["L0_conv_b1"].reshape(FT, 128).T), "b2": i["L0_conv_b2"],
        "ln_g": i["L0_conv_ln_g"], "ln_b": i["L0_conv_ln_b"], "ls": i["L0_conv_layer_scale"].reshape(C),
        "cb1": i["L0_conv_conv_b"],
        "t2": banded(i["L1_conv_conv_w"][:, 0], K2),
        "masks": np.stack([np.arange(3 * BC) >= BC, np.arange(3 * BC) >= 2 * BC], 1).astype(np.float32),
        "xproj": xproj, "dtw": dtw, "sel": sel,
        "ds": rows(i["L1_conv_Ds"]), "dt_bias": rows(i["L1_conv_dt_b"]), "cb2": rows(i["L1_conv_conv_b"]),
        "a_logs": rows(i["L1_conv_A_logs"]),
    }


def program(nc, groups, a, out):
    x1 = nc.dram_tensor("x1_dram", (IMAGES * C, L), F32, kind="Internal").ap()
    layer0(nc, groups, a["x"], a["t1"], a, x1)
    layer1(nc, groups, x1, a["t2"], a, out)


def kernel(**inputs):
    import concourse.bacc as bacc
    from concourse.bass_utils import run_bass_kernel_spmd

    nc = bacc.Bacc("TRN2", target_bir_lowering=False, num_devices=1)
    arrays = {name: np.ascontiguousarray(a) for name, a in lay_out({k: np.asarray(v) for k, v in inputs.items()}).items()}
    a = {name: nc.dram_tensor(f"in_{name}_dram", v.shape, mybir.dt.from_np(v.dtype), kind="ExternalInput").ap()
         for name, v in arrays.items()}
    out = nc.dram_tensor("out_dram", (IMAGES * C, L), F32, kind="ExternalOutput").ap()
    program(nc, GROUPS, a, out)
    r = run_bass_kernel_spmd(nc, [{f"in_{name}_dram": v for name, v in arrays.items()}], core_ids=[0])
    return r.results[0]["out_dram"].reshape(IMAGES, C, H, W)
```

```python
from contextlib import ExitStack

import numpy as np

import concourse.bass as bass
from concourse import mybir

F32 = mybir.dt.float32
F32R = mybir.dt.float32r
ALU = mybir.AluOpType
ACT = mybir.ActivationFunctionType
AX_X = mybir.AxisListType.X
ds = bass.ds

IMAGES, C, H, W = 32, 96, 56, 56
L = H * W
GI = 4
GROUPS = IMAGES // GI
ROWS = 2
TOK = ROWS * W
IMG_BLK = H // ROWS
BLOCKS = GI * IMG_BLK
BLKS = 4
BT = BLKS * TOK
BANDS = L // BT
UNITS = GI * BANDS
BANK = 512
CQ = 4
QUNITS = C // CQ
TW = 4

K1, PAD1 = 7, 3
COLS1 = W + 2 * PAD1
WIN1 = ROWS * COLS1
KT1 = (ROWS + K1 - 1) // ROWS
NWIN1 = (H + 2 * PAD1) // ROWS
TURNS1 = -(-NWIN1 // TW)
SLOTS1 = 6
FF = 4 * C
FT = FF // 128
LN_EPS = 1e-5
CHUNK = 7
CHUNKS = BLOCKS // CHUNK

K2, PAD2 = 5, 2
COLS2 = W + 2 * PAD2
WIN2 = ROWS * COLS2
KT2 = (ROWS + K2 - 1) // ROWS
NWIN2 = (H + 2 * PAD2) // ROWS
CB = 32
CBS = C // CB
TURNS2 = 2
TW2 = NWIN2 // TURNS2
SLOTS2 = 4
HALVES = 2
SLABS = 3
AHEAD = 5
ZSTEPS = 4
DA_SLOTS = 4
N, R = 4, 6
EPS = 1e-9
TILES = GI * C // 128
STEPS = TILES * N
XB = 32
DT0 = 4 * GI
XD = N * XB
assert GI == N and DT0 + 2 * R <= XB


def window_copy(win, ps_stage, n):
    i, part = n // TURNS1, n % TURNS1
    a, z = part * TW, min((part + 1) * TW, NWIN1)
    return (win[:, :, i, a:z].rearrange("p c w -> p w c"),
            ps_stage[n % 2][0:WIN1, 0:(z - a) * C].rearrange("p (w c) -> p w c", c=C))


def layer0(nc, groups, x, t1, consts, x1):
    xrow = x.rearrange("b c h w -> (b c) (h w)")
    ximg = x.rearrange("b c h w -> (b c) h w")
    with ExitStack() as ctx:
        def sb(name, shape, dt=F32):
            return ctx.enter_context(nc.sbuf_tensor(name, shape, dt))

        def pb(name):
            return ctx.enter_context(nc.psum_tensor(name, [128, BANK], F32))

        def sem(name):
            return ctx.enter_context(nc.semaphore(name))

        ident = sb("ident1", [128, 128])
        w1 = sb("w1", [C, FF])
        w2 = sb("w2", [128, FT, C])
        b1 = sb("b1", [128, FT])
        b2 = sb("b2", [C, 1])
        gain = sb("gain", [C, 1])
        shift = sb("shift", [C, 1])
        scale_col = sb("scale_col", [C, 1])
        scale_row = sb("scale_row", [128, C])
        bias_row = sb("bias_row", [TOK, C])
        xpad = [sb(f"xpad{i}", [C, H + 2 * PAD1, COLS1]) for i in range(2)]
        win = sb("win", [WIN1, C, GI, NWIN1])
        taps = [sb(f"taps1_{i}", [WIN1, CQ, KT1, TOK]) for i in range(SLOTS1)]
        conv = sb("conv1", [TOK, BLOCKS, C])
        sq = [sb(f"sq{i}", [TOK, CHUNK, C]) for i in range(2)]
        ln_sum = [sb(f"ln_sum{i}", [TOK, CHUNK]) for i in range(2)]
        ln_mean = [sb(f"ln_mean{i}", [TOK, CHUNK]) for i in range(2)]
        ln_ss = [sb(f"ln_ss{i}", [TOK, CHUNK]) for i in range(2)]
        ln_var = [sb(f"ln_var{i}", [TOK, CHUNK]) for i in range(2)]
        ln_rstd = [sb(f"ln_rstd{i}", [TOK, CHUNK]) for i in range(2)]
        minus_half = sb("minus_half", [TOK, CHUNK])
        hn = [sb(f"hn{i}", [C, BT]) for i in range(2)]
        act_h = [sb(f"act_h{i}", [128, FT, BT]) for i in range(2)]
        xres = [sb(f"xres{i}", [C, BT]) for i in range(2)]
        x1o = [sb(f"x1o{i}", [C, BT]) for i in range(2)]

        ps_stage = [pb(f"ps_stage{i}") for i in range(2)]
        ps_back = [pb(f"ps_back{i}") for i in range(2)]
        ps_up = [pb(f"ps_up{i}") for i in range(FT)]
        ps_down = pb("ps_down")

        consts_in = sem("consts_in")
        prepared = sem("prepared")
        xpad_ready = [sem(f"xpad_ready{i}") for i in range(2)]
        taps_ready = [sem(f"taps1_ready{i}") for i in range(SLOTS1)]
        xres_ready = [sem(f"xres_ready{i}") for i in range(2)]
        x1_stored = [sem(f"x1_stored{i}") for i in range(2)]
        win_turned = sem("win_turned")
        win_kept_dve = sem("win_kept_dve")
        win_kept_act = sem("win_kept_act")
        conv_done = sem("conv_done")
        conv_kept = sem("conv_kept")
        ln_summed = sem("ln_summed")
        ln_mean_ready = sem("ln_mean_ready")
        ln_centred = sem("ln_centred")
        ln_ss_ready = sem("ln_ss_ready")
        ln_var_ready = sem("ln_var_ready")
        ln_scaled = sem("ln_scaled")
        sq_ready = sem("sq_ready")
        rstd_ready = sem("rstd_ready")
        back_done = sem("back_done")
        hn_ready = sem("hn_ready")
        up_done = sem("up_done")
        gelu_done = sem("gelu_done")
        down_done = sem("down_done")
        x1_done = sem("x1_done")
        block = ctx.enter_context(nc.Block())

        first_unit = [c * CHUNK // BLKS for c in range(CHUNKS)]
        ln_at = {u: [] for u in range(UNITS)}
        for c in range(2, CHUNKS):
            ln_at[first_unit[c] - 3] += [(c, 0), (c, 1), (c, 2)]
            ln_at[first_unit[c] - 2] = [(c, 3), (c, 4), (c, 5)] + ln_at[first_unit[c] - 2]
        TURNS = GI * TURNS1
        TURN = {BANDS * (i - 1) + 3 + k: i * TURNS1 + 2 * k for i in range(1, GI) for k in range(TURNS1 // 2)}

        PREPARED = 4
        last = groups - 1

        @block.sync
        def _(sp):
            c = consts
            loads = [(ident[:, :], c["ident"]), (w1[:, :], c["w1"]),
                     (w2[:, :, :], c["w2"].rearrange("(t p) c -> p t c", p=128)),
                     (b1[:, :], c["b1"]),
                     (b2[:, :], c["b2"].rearrange("(p o) -> p o", o=1)),
                     (gain[:, :], c["ln_g"].rearrange("(p o) -> p o", o=1)),
                     (shift[:, :], c["ln_b"].rearrange("(p o) -> p o", o=1)),
                     (scale_col[:, :], c["ls"].rearrange("(p o) -> p o", o=1)),
                     (scale_row[:, :], c["ls"].partition_broadcast(128)),
                     (bias_row[:, :], c["cb1"].partition_broadcast(TOK))]
            for dst, src in loads:
                sp.dma_start(dst, src).then_inc(consts_in, 16)

            def load_image(f, i):
                sp.dma_start(xpad[i % 2][:, PAD1:PAD1 + H, PAD1:PAD1 + W],
                             ximg[ds((f * GI + i) * C, C), :, :]).then_inc(xpad_ready[i % 2], 16)

            def load_taps(q):
                slot = q % SLOTS1
                sp.dma_start(taps[slot][:, :, :, :], t1[q]).then_inc(taps_ready[slot], 16)

            def load_xres(f, u):
                sp.dma_start(xres[u % 2][:, :],
                             xrow[ds((f * GI + u // BANDS) * C, C), (u % BANDS) * BT:(u % BANDS + 1) * BT]
                             ).then_inc(xres_ready[u % 2], 16)

            sp.wait_ge(prepared, PREPARED)
            load_image(0, 0)
            load_image(0, 1)
            for q in range(SLOTS1):
                load_taps(q)
            load_xres(0, 0)
            load_xres(0, 1)
            for i in range(2, GI):
                sp.wait_ge(win_turned, TURNS1 * (i - 1))
                load_image(0, i)

            def group(g, more):
                if more:
                    sp.wait_ge(win_turned, (g + 1) * TURNS)
                    load_image(g + 1, 0)
                    load_image(g + 1, 1)
                for q in range(QUNITS):
                    if more or q + SLOTS1 < QUNITS:
                        sp.wait_ge(conv_done, g * QUNITS + q + 1)
                        load_taps((q + SLOTS1) % QUNITS)
                for u in range(UNITS):
                    if more and u in (BANDS, 2 * BANDS):
                        i = u // BANDS + 1
                        sp.wait_ge(win_turned, (g + 1) * TURNS + TURNS1 * (i - 1))
                        load_image(g + 1, i)
                    sp.wait_ge(x1_done, g * UNITS + u + 1)
                    sp.dma_start(x1[ds((g * GI + u // BANDS) * C, C), (u % BANDS) * BT:(u % BANDS + 1) * BT],
                                 x1o[u % 2][:, :]).then_inc(x1_stored[u % 2], 16)
                    if u + 2 < UNITS:
                        load_xres(g, u + 2)
                    elif more:
                        load_xres(g + 1, u + 2 - UNITS)

            if last:
                with sp.Fori(0, last) as g:
                    group(g, True)
            group(last, False)
            for p in range(2):
                sp.wait_ge(x1_stored[p], 16 * (groups * UNITS // 2 + 1))

        @block.gpsimd
        def _(pool):
            nc.gpsimd.memset(minus_half[:, :], -0.5).then_inc(prepared, 1)
            pool.sem_inc(x1_stored[0], 16)
            pool.sem_inc(x1_stored[1], 16)
            pool.wait_ge(prepared, PREPARED)

            def group(g):
                for c in range(CHUNKS):
                    pool.wait_ge(ln_var_ready, g * CHUNKS + c + 1)
                    nc.gpsimd.tensor_tensor(ln_rstd[c % 2][:, :], ln_var[c % 2][:, :], minus_half[:, :],
                                            ALU.pow).then_inc(rstd_ready, 1)

            with pool.Fori(0, groups) as g:
                group(g)

        @block.vector
        def _(dve):
            for p in range(2):
                nc.vector.memset(xpad[p][:, :, :], 0.0).then_inc(prepared, 1)
            dve.wait_ge(consts_in, 16 * 10)
            nc.vector.tensor_tensor(w2[:, :, :], w2[:, :, :],
                                    scale_row[:, :].unsqueeze(1).broadcast_to([128, FT, C]),
                                    ALU.mult)
            nc.vector.tensor_tensor(b2[:, :], b2[:, :], scale_col[:, :], ALU.mult).then_inc(prepared, 1)

            def keep_windows(f, n):
                dve.wait_ge(win_turned, f * TURNS + n + 1)
                nc.vector.tensor_copy(*window_copy(win, ps_stage, n)).then_inc(win_kept_dve, 1)

            def ln(g, c, step):
                n = g * CHUNKS + c + 1
                blocks = conv[:, c * CHUNK:(c + 1) * CHUNK, :]
                wide = [TOK, CHUNK, C]
                k = c % 2
                if step == 0:
                    nc.vector.tensor_reduce(ln_sum[k][:, :], blocks, AX_X, ALU.add).then_inc(ln_summed, 1)
                elif step == 1:
                    dve.wait_ge(ln_summed, n)
                    nc.vector.tensor_scalar(ln_mean[k][:, :], ln_sum[k][:, :], 1.0 / C, None,
                                            ALU.mult).then_inc(ln_mean_ready, 1)
                elif step == 2:
                    dve.wait_ge(ln_mean_ready, n)
                    nc.vector.tensor_tensor(blocks, blocks, ln_mean[k][:, :].unsqueeze(2).broadcast_to(wide),
                                            ALU.subtract).then_inc(ln_centred, 1)
                elif step == 3:
                    dve.wait_ge(sq_ready, n)
                    nc.vector.tensor_reduce(ln_ss[k][:, :], sq[k][:, :, :], AX_X, ALU.add).then_inc(ln_ss_ready, 1)
                elif step == 4:
                    dve.wait_ge(ln_ss_ready, n)
                    nc.vector.tensor_scalar(ln_var[k][:, :], ln_ss[k][:, :], 1.0 / C, LN_EPS, ALU.mult,
                                            ALU.add).then_inc(ln_var_ready, 1)
                else:
                    dve.wait_ge(rstd_ready, n)
                    nc.vector.tensor_tensor(blocks, blocks, ln_rstd[k][:, :].unsqueeze(2).broadcast_to(wide),
                                            ALU.mult).then_inc(ln_scaled, 1)

            def normed(g, u):
                dve.wait_ge(back_done, g * UNITS + u + 1)
                nc.vector.tensor_scalar(hn[u % 2][:, :], ps_back[u % 2][0:C, 0:BT], gain[:, 0:1], shift[:, 0:1],
                                        ALU.mult, ALU.add).then_inc(hn_ready, 1)

            def residual(g, u):
                dve.wait_ge(down_done, g * UNITS + u + 1)
                dve.wait_ge(xres_ready[u % 2], (g * (UNITS // 2) + u // 2 + 1) * 16)
                dve.wait_ge(x1_stored[u % 2], (g * (UNITS // 2) + u // 2 + 1) * 16)
                nc.vector.scalar_tensor_tensor(x1o[u % 2][:, :], ps_down[0:C, 0:BT], b2[:, 0:1],
                                               xres[u % 2][:, :], ALU.add, ALU.add).then_inc(x1_done, 1)

            def group(g, more):
                for q in range(QUNITS):
                    dve.wait_ge(conv_done, g * QUNITS + q + 1)
                    nc.vector.tensor_tensor(
                        conv[:, :, q * CQ:(q + 1) * CQ].rearrange("p b c -> p c b"),
                        ps_stage[q % 2][0:TOK, 0:CQ * BLOCKS].rearrange("p (c b) -> p c b", c=CQ),
                        bias_row[:, q * CQ:(q + 1) * CQ].unsqueeze(2).broadcast_to([TOK, CQ, BLOCKS]),
                        ALU.add).then_inc(conv_kept, 1)
                dve.wait_ge(conv_kept, g * QUNITS + QUNITS)
                for c, step in ((0, 0), (0, 1), (1, 0), (0, 2), (1, 1), ("windows", 0), (0, 3), (0, 4), (1, 2),
                                ("windows", 2), (0, 5), ("windows", 4)):
                    if c != "windows":
                        ln(g, c, step)
                    elif more:
                        keep_windows(g + 1, step)
                normed(g, 0)
                for step in (3, 4, 5):
                    ln(g, 1, step)
                if more:
                    keep_windows(g + 1, 6)
                for u in range(UNITS):
                    if u + 1 < UNITS:
                        normed(g, u + 1)
                    if more and u in TURN:
                        keep_windows(g + 1, TURN[u])
                    for c, step in ln_at[u]:
                        if step not in (2, 5):
                            ln(g, c, step)
                    if u > 0:
                        residual(g, u - 1)
                    for c, step in ln_at[u]:
                        if step in (2, 5):
                            ln(g, c, step)
                residual(g, UNITS - 1)

            for n in range(0, TURNS, 2):
                keep_windows(0, n)
            if last:
                with dve.Fori(0, last) as g:
                    group(g, True)
            group(last, False)

        @block.scalar
        def _(act):
            def keep_windows(f, n):
                act.wait_ge(win_turned, f * TURNS + n + 1)
                nc.scalar.activation(*window_copy(win, ps_stage, n), ACT.Copy).then_inc(win_kept_act, 1)

            def square(g, c):
                act.wait_ge(ln_centred, g * CHUNKS + c + 1)
                nc.scalar.activation(sq[c % 2][:, :, :], conv[:, c * CHUNK:(c + 1) * CHUNK, :],
                                     ACT.Square).then_inc(sq_ready, 1)

            def gelu(g, u):
                if u >= 2:
                    act.wait_ge(down_done, g * UNITS + u - 1)
                for t in range(FT):
                    act.wait_ge(up_done, (g * UNITS + u) * FT + t + 1)
                    nc.scalar.activation(act_h[u % 2][:, t, :], ps_up[t][:, 0:BT], ACT.Gelu,
                                         bias=b1[:, t:t + 1]).then_inc(gelu_done, 1)

            def group(g, more):
                if more:
                    keep_windows(g + 1, 1)
                square(g, 0)
                if more:
                    keep_windows(g + 1, 3)
                square(g, 1)
                if more:
                    for n in (5, 7):
                        keep_windows(g + 1, n)
                for u in range(UNITS):
                    gelu(g, u)
                    if more and u in TURN:
                        keep_windows(g + 1, TURN[u] + 1)
                    for c in range(2, CHUNKS):
                        if first_unit[c] - 3 == u:
                            square(g, c)

            act.wait_ge(consts_in, 16 * 10)
            for n in range(1, TURNS, 2):
                keep_windows(0, n)
            if last:
                with act.Fori(0, last) as g:
                    group(g, True)
            group(last, False)

        @block.tensor
        def _(pe):
            def turn_windows(f, first, n):
                i, part = n // TURNS1, n % TURNS1
                if part == 0:
                    pe.wait_ge(xpad_ready[i % 2], (f * (GI // 2) + i // 2 + 1) * 16)
                if n >= 2:
                    pe.wait_ge((win_kept_dve, win_kept_act)[n % 2], f * (TURNS // 2) + n // 2)
                elif not first:
                    pe.wait_ge(conv_kept, f * QUNITS)
                pixels = xpad[i % 2][:, :, :].rearrange("p r w -> p (r w)")
                for j, w in enumerate(range(part * TW, min((part + 1) * TW, NWIN1))):
                    mm = nc.tensor.transpose(ps_stage[n % 2][0:WIN1, j * C:(j + 1) * C],
                                             pixels[:, w * WIN1:(w + 1) * WIN1], ident[0:C, 0:C])
                mm.then_inc(win_turned, 1)

            def convolve(g):
                pe.wait_ge(win_kept_dve, (g + 1) * (TURNS // 2))
                pe.wait_ge(win_kept_act, (g + 1) * (TURNS // 2))
                for q in range(QUNITS):
                    pe.wait_ge(taps_ready[q % SLOTS1], (g * (QUNITS // SLOTS1) + q // SLOTS1 + 1) * 16)
                    if q >= 2:
                        pe.wait_ge(conv_kept, g * QUNITS + q - 1)
                    for c in range(CQ):
                        for k in range(KT1):
                            mm = nc.tensor.matmul(
                                ps_stage[q % 2][0:TOK, c * BLOCKS:(c + 1) * BLOCKS],
                                taps[q % SLOTS1][:, c, k, :],
                                win[:, q * CQ + c, :, k:k + IMG_BLK],
                                start=(k == 0), stop=(k == KT1 - 1))
                    mm.then_inc(conv_done, 1)

            def back(g, u):
                pe.wait_ge(ln_scaled, g * CHUNKS + (u * BLKS + BLKS - 1) // CHUNK + 1)
                if u >= 2:
                    pe.wait_ge(hn_ready, g * UNITS + u - 1)
                for j in range(BLKS):
                    mm = nc.tensor.transpose(ps_back[u % 2][0:C, j * TOK:(j + 1) * TOK],
                                             conv[:, u * BLKS + j, :], ident[0:TOK, 0:TOK])
                mm.then_inc(back_done, 1)

            def up(g, u):
                pe.wait_ge(hn_ready, g * UNITS + u + 1)
                for t in range(FT):
                    if u > 0:
                        pe.wait_ge(gelu_done, (g * UNITS + u - 1) * FT + t + 1)
                    nc.tensor.matmul(ps_up[t][:, 0:BT], w1[:, t * 128:(t + 1) * 128], hn[u % 2][:, :],
                                     start=True, stop=True).then_inc(up_done, 1)

            def down(g, u):
                pe.wait_ge(gelu_done, (g * UNITS + u + 1) * FT)
                if u > 0:
                    pe.wait_ge(x1_done, g * UNITS + u)
                for t in range(FT):
                    mm = nc.tensor.matmul(ps_down[0:C, 0:BT], w2[:, t, :], act_h[u % 2][:, t, :],
                                          start=(t == 0), stop=(t == FT - 1))
                mm.then_inc(down_done, 1)

            def group(g, more):
                convolve(g)
                if more:
                    for n in range(TURNS1):
                        turn_windows(g + 1, False, n)
                back(g, 0)
                for u in range(UNITS):
                    up(g, u)
                    if u + 1 < UNITS:
                        back(g, u + 1)
                    if more and u in TURN:
                        turn_windows(g + 1, False, TURN[u])
                        turn_windows(g + 1, False, TURN[u] + 1)
                    if u > 0:
                        down(g, u - 1)
                down(g, UNITS - 1)

            pe.wait_ge(consts_in, 16 * 10)
            pe.wait_ge(prepared, PREPARED)
            for n in range(TURNS):
                turn_windows(0, True, n)
            if last:
                with pe.Fori(0, last) as g:
                    group(g, True)
            group(last, False)


def layer1(nc, groups, x1, t2, consts, out):
    x1img = x1.rearrange("r (h w) -> r h w", h=H)
    with ExitStack() as ctx:
        def sb(name, shape, dt=F32):
            return ctx.enter_context(nc.sbuf_tensor(name, shape, dt))

        def pb(name):
            return ctx.enter_context(nc.psum_tensor(name, [128, BANK], F32))

        def sem(name):
            return ctx.enter_context(nc.semaphore(name))

        ident = sb("ident2", [128, 128])
        xproj = sb("xproj", [128, TILES, XD])
        dtw = [sb(f"dtw_{part}", [XD, TILES, 128], F32R) for part in ("high", "low")]
        sel = sb("sel", [XD, 2, TILES, 128], F32R)
        low_rows = sb("low_rows", [XD, 1])
        skip = sb("skip", [128, TILES, 128])
        ds_col = sb("ds_col", [128, TILES])
        dt_bias = sb("dt_bias", [128, TILES])
        conv_bias = sb("conv_bias", [128, TILES])
        a_neg = sb("a_neg", [128, TILES, N])
        zeros = sb("zeros", [128, STEPS])
        q_first = sb("q_first", [128, STEPS])
        xpad = sb("x1pad", [C, H + 2 * PAD2, COLS2])
        win = sb("win2", [WIN2, CB, GI, NWIN2])
        taps = [sb(f"taps2_{i}", [WIN2, CQ, KT2, TOK]) for i in range(SLOTS2)]
        conv = sb("conv2", [TOK, IMG_BLK, GI * C])
        xs = sb("xs", [128, TILES, L])
        xd = sb("xd", [XD, BT])
        high = sb("high", [XD, BT], F32R)
        parts = [sb(f"parts{i}", [XD, BT], F32R) for i in range(3)]
        z_pos = sb("z_pos", [128, TILES, BT])
        z_log = sb("z_log", [128, TILES, BT])
        delta = sb("delta", [128, TILES, BT])
        dxs = sb("dxs", [128, TILES, BT])
        d_a = [sb(f"d_a{i}", [128, BT]) for i in range(DA_SLOTS)]
        q = [sb(f"q{i}", [128, BT]) for i in range(2)]
        u = [sb(f"u{i}", [128, BT]) for i in range(2)]
        h = [sb(f"h{i}", [128, BT]) for i in range(2)]
        hc = [sb(f"hc{i}", [128, BT]) for i in range(2)]
        q_last = sb("q_last", [128, STEPS])
        h_last = sb("h_last", [128, STEPS])
        y = [sb(f"y{i}", [128, BT]) for i in range(2)]

        ps_front = [pb(f"ps_front{i}") for i in range(2)]
        ps_prep = [pb(f"ps_prep{i}") for i in range(2)]
        ps_b = pb("ps_b")
        ps_c = pb("ps_c")
        ps_y = [pb(f"ps_y{i}") for i in range(2)]

        consts_in = sem("consts2_in")
        prepared = sem("prepared2")
        slab_ready = [sem(f"slab_ready{i}") for i in range(SLABS)]
        taps_ready = [sem(f"taps2_ready{i}") for i in range(SLOTS2)]
        front_done = sem("front_done")
        front_kept = sem("front_kept")
        back_done = sem("back2_done")
        xs_kept = sem("xs_kept")
        xd_done = sem("xd_done")
        xd_ready = sem("xd_ready")
        parts_ready = sem("parts_ready")
        z_done = sem("z_done")
        dtw_high = sem("dtw_high")
        a_ready = sem("a_ready")
        z_step = sem("z_step")
        delta_ready = sem("delta_ready")
        dxs_ready = sem("dxs_ready")
        d_a_ready = sem("d_a_ready")
        b_ready = sem("b_ready")
        c_ready = sem("c_ready")
        clamp_done = sem("clamp_done")
        q_done = sem("q_done")
        u_done = sem("u_done")
        gated = sem("gated")
        h_done = sem("h_done")
        hc_done = sem("hc_done")
        q_kept = sem("q_kept")
        h_kept = sem("h_kept")
        y_done = sem("y_done")
        y_kept = sem("y_kept")
        y_stored = [sem(f"y_stored{i}") for i in range(2)]
        block = ctx.enter_context(nc.Block())

        last = groups - 1
        CONSTS = 16 * 9
        PREPARED = 3 + TILES + 3
        S = BANDS * STEPS
        RUNS = BANDS * TILES
        FRONT = CBS * (GI * TURNS2 + CB // CQ)
        units = []
        for cb in range(CBS):
            units += [("turn", cb, i, p) for i in range(GI) for p in range(TURNS2)]
            units += [("conv", cb, cu, 0) for cu in range(CB // CQ)]
        pieces = [(i, piece) for i in range(FRONT) for piece in range(1 if units[i][0] == "turn" else HALVES)]
        assert len(pieces) <= S - STEPS
        last_piece = {i: s for s, (i, _) in enumerate(pieces)}
        step_of = [s for s, (i, piece) in enumerate(pieces) if piece == 0]
        turn_unit = [units.index(("turn", k // GI, k % GI, TURNS2 - 1)) for k in range(CBS * GI)]
        conv_unit = [units.index(("conv", k // (CB // CQ), k % (CB // CQ), 0)) for k in range(QUNITS)]

        back_at = {1: range(0, 4), 2: range(4, 6), 7: range(6, 10), 8: range(10, 13),
                   10: range(13, 17), 11: range(17, 21)}
        silu_at = {1: (0, 6), 8: (6, 13), 11: (13, 21)}
        back_banks = ps_prep + ps_front

        PROJECT_AT = (0, 1, 2)
        XD_AT = 3
        SPLIT_AT = 4
        DELTA_AT = (4, 5, 6)
        Z_AT = (5, 6, 7)
        SUM_AT = (7, 9, 11)

        def parts_slot(b):
            return 2 if b == 0 else b % 2

        def next_band(g, b):
            return (g, b + 1) if b + 1 < BANDS else (g + 1, 0)

        @block.sync
        def _(sp):
            for dst, src in [(ident[:, :], consts["ident"]), (xproj[:, :, :], consts["xproj"]),
                             (xs[:, 0, 0:2 * TILES * 128], consts["sel"]),
                             (xs[:, 1, 0:TILES * 128], consts["dtw"]),
                             (ds_col[:, :], consts["ds"]), (dt_bias[:, :], consts["dt_bias"]),
                             (conv_bias[:, :], consts["cb2"]), (low_rows[:, :], consts["low_rows"]),
                             (a_neg[:, :, :], consts["a_logs"])]:
                sp.dma_start(dst, src).then_inc(consts_in, 16)

            def load_slab(f, first, k):
                if k >= SLABS:
                    sp.wait_ge(front_done, f * FRONT + turn_unit[k - SLABS] + 1)
                elif not first:
                    sp.wait_ge(front_done, (f - 1) * FRONT + turn_unit[k - SLABS] + 1)
                rows = slice(CB * (k % SLABS), CB * (k % SLABS) + CB)
                sp.dma_start(xpad[rows, PAD2:PAD2 + H, PAD2:PAD2 + W],
                             x1img[ds((f * GI + k % GI) * C + CB * (k // GI), CB), :, :]
                             ).then_inc(slab_ready[k % SLABS], 16)

            def load_taps(f, first, k):
                if k >= SLOTS2:
                    sp.wait_ge(front_done, f * FRONT + conv_unit[k - SLOTS2] + 1)
                elif not first:
                    sp.wait_ge(front_done, (f - 1) * FRONT + conv_unit[k - SLOTS2] + 1)
                sp.dma_start(taps[k % SLOTS2][:, :, :, :], t2[k]).then_inc(taps_ready[k % SLOTS2], 16)

            loads = []
            for cb in range(CBS):
                loads += [(load_slab, GI * cb + i, turn_unit[GI * cb + i]) for i in range(GI)]
                loads += [(load_taps, k, conv_unit[k]) for k in range(cb * CB // CQ, (cb + 1) * CB // CQ)]

            sp.wait_ge(prepared, PREPARED)
            for load, k, _ in loads:
                load(0, True, k)

            def store(g, r):
                b, t = r // TILES, r % TILES
                sp.wait_ge(y_kept, g * RUNS + r + 2)
                sp.dma_start(out[ds(g * GI * C + t * 128, 128), b * BT:(b + 1) * BT],
                             y[r % 2][:, :]).then_inc(y_stored[r % 2], 16)

            def group(g, more):
                todo = list(loads) if more else []
                for s in range(S):
                    while todo and step_of[todo[0][2]] <= s + AHEAD:
                        load, k, _ = todo.pop(0)
                        load(g + 1, False, k)
                    if s >= N + 2 and (s - N - 2) % N == 0:
                        store(g, (s - N - 2) // N)
                store(g, RUNS - 1)

            if last:
                with sp.Fori(0, last) as g:
                    group(g, True)
            group(last, False)
            for p in range(2):
                sp.wait_ge(y_stored[p], (groups * ((RUNS + 1 - p) // 2) + 1) * 16)

        @block.gpsimd
        def _(pool):
            nc.gpsimd.memset(xpad[:, :, :], 0.0).then_inc(prepared, 1)
            nc.gpsimd.memset(zeros[:, :], 0.0).then_inc(prepared, 1)
            nc.gpsimd.memset(q_first[:, :], float(np.float32(1) / np.float32(EPS))).then_inc(prepared, 1)
            pool.sem_inc(y_stored[0], 16)
            pool.sem_inc(y_stored[1], 16)
            pool.sem_inc(y_kept, 1)
            pool.wait_ge(prepared, PREPARED)

            def add(o, a, b):
                return nc.gpsimd.tensor_tensor(o, a, b, ALU.add)

            def split(f, b):
                pool.wait_ge(xd_ready, (f * BANDS + b + 1) * 2)
                nc.gpsimd.tensor_tensor(parts[parts_slot(b)][:, :], xd[:, :], high[:, :],
                                        ALU.subtract).then_inc(parts_ready, 1)

            def sum_delta(f, b, t, first=False):
                pool.wait_ge(z_step, (f * RUNS + b * TILES + t + 1) * ZSTEPS)
                if not first:
                    pool.wait_ge(d_a_ready, (f * BANDS + b - 1) * STEPS + (t + 1) * N)
                    pool.wait_ge(u_done, (f * BANDS + b - 1) * STEPS + (t + 1) * N)
                add(delta[:, t, :], z_pos[:, t, :], z_log[:, t, :]).then_inc(delta_ready, 1)

            def times_x(f, b, t):
                pool.wait_ge(delta_ready, f * RUNS + b * TILES + t + 1)
                nc.gpsimd.tensor_tensor(dxs[:, t, :], delta[:, t, :], xs[:, t, b * BT:(b + 1) * BT],
                                        ALU.mult).then_inc(dxs_ready, 1)

            def group(g, more):
                for s in range(S):
                    b, j = s // STEPS, s % STEPS
                    f, fb = next_band(g, b)
                    prepare = more or b + 1 < BANDS
                    pool.wait_ge(q_done, g * S + s + 1)
                    q_from = q[s % 2][:, BT - 1:BT] if b + 1 < BANDS else q_first[:, 0:1]
                    add(q_last[:, j:j + 1], q_from, zeros[:, 0:1]).then_inc(q_kept, 1)
                    if prepare and j == SPLIT_AT:
                        split(f, fb)
                    if prepare and j in SUM_AT:
                        sum_delta(f, fb, SUM_AT.index(j))
                    if prepare and j - 1 in SUM_AT:
                        times_x(f, fb, SUM_AT.index(j - 1))
                    pool.wait_ge(h_done, g * S + s + 1)
                    h_from = h[s % 2][:, BT - 1:BT] if b + 1 < BANDS else zeros[:, 0:1]
                    add(h_last[:, j:j + 1], h_from, zeros[:, 0:1]).then_inc(h_kept, 1)
                    if prepare and j == STEPS - 1:
                        times_x(f, fb, TILES - 1)

            add(q_last[:, :], q_first[:, :], zeros[:, :]).then_inc(q_kept, STEPS)
            add(h_last[:, :], zeros[:, :], zeros[:, :]).then_inc(h_kept, STEPS)
            split(0, 0)
            for t in range(TILES):
                sum_delta(0, 0, t, True)
                times_x(0, 0, t)
            if last:
                with pool.Fori(0, last) as g:
                    group(g, True)
            group(last, False)

        @block.vector
        def _(dve):
            dve.wait_ge(consts_in, CONSTS)
            staged = xs[:, 1, 0:TILES * 128].rearrange("p (t q) -> p t q", t=TILES)
            nc.vector.tensor_copy(sel[:, :, :, :].rearrange("p k t q -> p (k t q)"),
                                  xs[:, 0, 0:2 * TILES * 128]).then_inc(prepared, 1)
            nc.vector.tensor_copy(dtw[0][:, :, :], staged).then_inc(dtw_high, 1)
            for t in range(TILES):
                nc.vector.tensor_scalar(skip[:, t, :], ident[:, :], ds_col[:, t:t + 1], None,
                                        ALU.mult).then_inc(prepared, 1)
            dve.wait_ge(dtw_high, 1)
            nc.vector.tensor_tensor(dtw[1][:, :, :], staged, dtw[0][:, :, :], ALU.subtract).then_inc(prepared, 1)
            dve.wait_ge(a_ready, 1)
            nc.vector.tensor_scalar(a_neg[:, :, :], a_neg[:, :, :], -1.0, None, ALU.mult).then_inc(prepared, 1)

            def clamp(n, j):
                dve.wait_ge(d_a_ready, n + j + 1)
                nc.vector.tensor_scalar(d_a[j % DA_SLOTS][:, :], d_a[j % DA_SLOTS][:, :], float(np.float32(EPS)), None,
                                        ALU.max).then_inc(clamp_done, 1)

            def times_b(n, runs, j):
                dve.wait_ge(b_ready, n + j + 1)
                if j % N == 0:
                    dve.wait_ge(dxs_ready, runs + j // N + 1)
                nc.vector.tensor_tensor(u[j % 2][:, :], dxs[:, j // N, :], ps_b[:, 0:BT], ALU.mult).then_inc(u_done, 1)

            def scan_q(n, kept, j):
                dve.wait_ge(clamp_done, n + j + 1)
                dve.wait_ge(q_kept, kept + j)
                nc.vector.tensor_tensor_scan(q[j % 2][:, :], d_a[j % DA_SLOTS][:, :], zeros[:, 0:1].broadcast_to([128, BT]), q_last[:, j:j + 1],
                                             ALU.mult, ALU.add).then_inc(q_done, 1)

            def gate(n, j):
                dve.wait_ge(q_done, n + j + 1)
                dve.wait_ge(u_done, n + j + 1)
                nc.vector.scalar_tensor_tensor(u[j % 2][:, :], q[j % 2][:, :], 1.0, u[j % 2][:, :],
                                               ALU.min, ALU.mult).then_inc(gated, 1)

            def scan_h(n, kept, j):
                dve.wait_ge(gated, n + j + 1)
                dve.wait_ge(h_kept, kept + j)
                nc.vector.tensor_tensor_scan(h[j % 2][:, :], d_a[j % DA_SLOTS][:, :], u[j % 2][:, :], h_last[:, j:j + 1],
                                             ALU.mult, ALU.add).then_inc(h_done, 1)

            def times_c(n, j):
                dve.wait_ge(h_done, n + j + 1)
                dve.wait_ge(c_ready, n + j + 1)
                nc.vector.tensor_tensor(hc[j % 2][:, :], h[j % 2][:, :], ps_c[:, 0:BT], ALU.mult).then_inc(hc_done, 1)

            with dve.Fori(0, groups) as g:
                with dve.Fori(0, BANDS) as b:
                    n = g * S + b * STEPS
                    runs = g * RUNS + b * TILES
                    kept = n + STEPS - 1
                    clamp(n, 0)
                    times_b(n, runs, 0)
                    for j in range(STEPS):
                        scan_q(n, kept, j)
                        if j > 0:
                            times_c(n, j - 1)
                        gate(n, j)
                        if j + 1 < STEPS:
                            clamp(n, j + 1)
                        scan_h(n, kept, j)
                        if j + 1 < STEPS:
                            times_b(n, runs, j + 1)
                    times_c(n, STEPS - 1)

        @block.scalar
        def _(act):
            def keep_front(f, i):
                kind, cb, k, p = units[i]
                act.wait_ge(front_done, f * FRONT + i + 1)
                if kind == "turn":
                    src = ps_front[i % 2][0:WIN2, 0:TW2 * CB].rearrange("p (w c) -> p w c", c=CB)
                    dst = win[:, :, k, p * TW2:(p + 1) * TW2].rearrange("p c w -> p w c")
                else:
                    c0 = cb * CB + k * CQ
                    src = ps_front[i % 2][0:TOK, 0:CQ * BLOCKS].rearrange("p (c i b) -> p c i b", c=CQ, i=GI)
                    dst = conv[:, :, :].rearrange("p b (i c) -> p c i b", i=GI)[:, c0:c0 + CQ, :, :]
                nc.scalar.activation(dst, src, ACT.Copy).then_inc(front_kept, 1)

            def silus(f, lo, hi):
                act.preload_act_table_set("silu_and_others")
                for r in range(lo, hi):
                    b, t = r // TILES, r % TILES
                    act.wait_ge(back_done, f * RUNS + r + 1)
                    nc.scalar.activation(xs[:, t, b * BT:(b + 1) * BT], back_banks[r % 4][:, 0:BT], ACT.Silu,
                                         bias=conv_bias[:, t:t + 1]).then_inc(xs_kept, 1)
                act.preload_act_table_set("natural_log_exp_and_others")

            def keep_xd(f, b, first=False):
                act.wait_ge(xd_done, f * BANDS + b + 1)
                if not first:
                    act.wait_ge(parts_ready, f * BANDS + b)
                nc.scalar.activation(xd[:, :], ps_prep[0][:, 0:BT], ACT.Copy).then_inc(xd_ready, 1)
                nc.scalar.activation(high[:, :], ps_prep[0][:, 0:BT], ACT.Identity,
                                     scale=low_rows[:, 0:1]).then_inc(xd_ready, 1)

            def softplus(f, b, t, late, first=False):
                n = (f * RUNS + b * TILES + t) * ZSTEPS
                bias = dt_bias[:, t:t + 1]
                if late:
                    act.wait_ge(z_step, n + 3)
                    nc.scalar.activation(z_log[:, t, :], z_log[:, t, :], ACT.Ln, bias=1.0).then_inc(z_step, 1)
                    return
                act.wait_ge(z_done, f * RUNS + b * TILES + t + 1)
                if not first:
                    act.wait_ge(delta_ready, f * RUNS + (b - 1) * TILES + t + 1)
                src = ps_prep[(1 + t) % 2][:, 0:BT]
                nc.scalar.activation(z_log[:, t, :], src, ACT.Abs, bias=bias).then_inc(z_step, 1)
                nc.scalar.activation(z_pos[:, t, :], src, ACT.Relu, bias=bias).then_inc(z_step, 1)
                act.wait_ge(z_step, n + 2)
                nc.scalar.activation(z_log[:, t, :], z_log[:, t, :], ACT.Exp, scale=-1.0).then_inc(z_step, 1)

            def exp_a(g, s, first=False):
                b, t, n = s % S // STEPS, s % STEPS // N, s % N
                if n == 0:
                    act.wait_ge(delta_ready, g * RUNS + s // N + 1)
                if not first:
                    act.wait_ge(h_done, g * S + s - DA_SLOTS + 1)
                nc.scalar.activation(d_a[s % DA_SLOTS][:, :], delta[:, t, :], ACT.Exp,
                                     scale=a_neg[:, t, n:n + 1]).then_inc(d_a_ready, 1)

            def keep_y(g, r):
                act.wait_ge(y_done, g * RUNS + r + 1)
                act.wait_ge(y_stored[r % 2], (g * ((RUNS + 1 - r % 2) // 2) + r // 2 + 1) * 16)
                nc.scalar.activation(y[r % 2][:, :], ps_y[r % 2][:, 0:BT], ACT.Copy).then_inc(y_kept, 1)

            def group(g, more):
                for s in range(S):
                    b, j = s // STEPS, s % STEPS
                    f, fb = next_band(g, b)
                    if more or s + DA_SLOTS - 1 < S:
                        exp_a(g, s + DA_SLOTS - 1)
                    if more and s - 1 in last_piece.values():
                        keep_front(g + 1, pieces[s - 1][0])
                    if s >= N + 1 and (s - N - 1) % N == 0:
                        keep_y(g, (s - N - 1) // N)
                    if more or b + 1 < BANDS:
                        if j == XD_AT + (b + 1 == BANDS):
                            keep_xd(f, fb)
                        if j - 1 in Z_AT:
                            softplus(f, fb, Z_AT.index(j - 1), True)
                        if j in Z_AT:
                            softplus(f, fb, Z_AT.index(j), False)
                    if more and b + 1 == BANDS and j in silu_at:
                        silus(f, *silu_at[j])
                keep_y(g, RUNS - 1)

            act.preload_act_table_set("natural_log_exp_and_others")
            act.wait_ge(consts_in, CONSTS)
            nc.scalar.activation(a_neg[:, :, :], a_neg[:, :, :], ACT.Exp).then_inc(a_ready, 1)
            act.wait_ge(prepared, PREPARED)
            for i in range(FRONT):
                keep_front(0, i)
            silus(0, 0, RUNS)
            keep_xd(0, 0, True)
            for t in range(TILES):
                softplus(0, 0, t, False, True)
                softplus(0, 0, t, True, True)
            for s in range(DA_SLOTS - 1):
                exp_a(0, s, True)
            if last:
                with act.Fori(0, last) as g:
                    group(g, True)
            group(last, False)

        @block.tensor
        def _(pe):
            def front_waits(f, i, first=False):
                kind, cb, k, p = units[i]
                if i < 2 and not first:
                    pe.wait_ge(xs_kept, f * RUNS)
                if kind == "turn":
                    slab = cb * GI + k
                    pe.wait_ge(slab_ready[slab % SLABS], (f * (CBS * GI // SLABS) + slab // SLABS + 1) * 16)
                    if i >= 2:
                        pe.wait_ge(front_kept, f * FRONT + i - 1)
                else:
                    n = cb * (CB // CQ) + k
                    pe.wait_ge(taps_ready[n % SLOTS2], (f * (QUNITS // SLOTS2) + n // SLOTS2 + 1) * 16)
                    pe.wait_ge(front_kept, f * FRONT + (i if k == 0 else i - 1))

            def front(i, piece):
                kind, cb, k, p = units[i]
                if kind == "turn":
                    slab = cb * GI + k
                    rows = slice(CB * (slab % SLABS), CB * (slab % SLABS) + CB)
                    pixels = xpad[rows, :, :].rearrange("p r w -> p (r w)")
                    for w in range(TW2):
                        mm = nc.tensor.transpose(ps_front[i % 2][0:WIN2, w * CB:(w + 1) * CB],
                                                 pixels[:, (p * TW2 + w) * WIN2:(p * TW2 + w + 1) * WIN2],
                                                 ident[rows, rows])
                else:
                    n = cb * (CB // CQ) + k
                    for c in range(piece * CQ // HALVES, (piece + 1) * CQ // HALVES):
                        for w in range(KT2):
                            mm = nc.tensor.matmul(
                                ps_front[i % 2][0:TOK, c * BLOCKS:(c + 1) * BLOCKS],
                                taps[n % SLOTS2][:, c, w, :],
                                win[:, k * CQ + c, :, w:w + IMG_BLK],
                                start=(w == 0), stop=(w == KT2 - 1))
                if kind == "turn" or piece == HALVES - 1:
                    mm.then_inc(front_done, 1)

            def back(f, r, first=False):
                b, t = r // TILES, r % TILES
                if r == 0:
                    pe.wait_ge(front_kept, (f + 1) * FRONT)
                if r == 0 and not first:
                    pe.wait_ge(z_step, (f * RUNS - 1) * ZSTEPS + 2)
                if r in (8, 9) and not first:
                    pe.wait_ge(z_step, (f * RUNS + r - 7) * ZSTEPS + 2)
                if r >= 4:
                    pe.wait_ge(xs_kept, f * RUNS + r - 3)
                for j in range(BLKS):
                    mm = nc.tensor.transpose(back_banks[r % 4][:, j * TOK:(j + 1) * TOK],
                                             conv[:, b * BLKS + j, t * 128:(t + 1) * 128], ident[0:TOK, 0:TOK])
                mm.then_inc(back_done, 1)

            def project(f, b, t, first=False):
                if t == 0 and b < 2:
                    pe.wait_ge(xs_kept, f * RUNS + (RUNS if b or first else silu_at[1][1]))
                if t == 0 and b > 0:
                    pe.wait_ge(z_step, (f * RUNS + (b - 1) * TILES + 1) * ZSTEPS + 2)
                mm = nc.tensor.matmul(ps_prep[0][:, 0:BT], xproj[:, t, :], xs[:, t, b * BT:(b + 1) * BT],
                                      start=(t == 0), stop=(t == TILES - 1))
                if t == TILES - 1:
                    mm.then_inc(xd_done, 1)

            def delta_rows(f, b, t):
                if t == 0:
                    pe.wait_ge(parts_ready, f * BANDS + b + 1)
                else:
                    pe.wait_ge(z_step, (f * RUNS + b * TILES + t - 1) * ZSTEPS + 2)
                bank = ps_prep[(1 + t) % 2]
                for part in range(2):
                    mm = nc.tensor.matmul(bank[:, 0:BT], dtw[part][:, t, :], parts[parts_slot(b)][:, :],
                                          start=(part == 0), stop=(part == 1))
                mm.then_inc(z_done, 1)

            def spread(bank, which, s):
                b, t, n = s // STEPS, s % STEPS // N, s % N
                rows = slice(n * XB, (n + 1) * XB)
                return nc.tensor.matmul(bank[:, 0:BT], sel[rows, which, t, :], parts[parts_slot(b)][rows, :],
                                        start=True, stop=True)

            def spread_b(g, s, first=False):
                if s % STEPS == 0:
                    pe.wait_ge(parts_ready, g * BANDS + s // STEPS + 1)
                if not first:
                    pe.wait_ge(u_done, g * S + s)
                spread(ps_b, 0, s % S).then_inc(b_ready, 1)

            def spread_c(g, s, first=False):
                if not first:
                    pe.wait_ge(hc_done, g * S + s)
                spread(ps_c, 1, s).then_inc(c_ready, 1)

            def add_y(g, s):
                b, t, n = s // STEPS, s % STEPS // N, s % N
                r = b * TILES + t
                if n == 0:
                    if r != 1:
                        pe.wait_ge(y_kept, g * RUNS + max(r - 1, 0) + 1)
                    nc.tensor.matmul(ps_y[r % 2][:, 0:BT], skip[:, t, :], xs[:, t, b * BT:(b + 1) * BT],
                                     start=True, stop=False)
                pe.wait_ge(hc_done, g * S + s + 1)
                mm = nc.tensor.matmul(ps_y[r % 2][:, 0:BT], ident[:, :], hc[s % 2][:, :],
                                      start=False, stop=(n == N - 1))
                if n == N - 1:
                    mm.then_inc(y_done, 1)

            def group(g, more):
                for s in range(S):
                    b, j = s // STEPS, s % STEPS
                    f, fb = next_band(g, b)
                    if more and s < len(pieces) and pieces[s][1] == 0:
                        front_waits(g + 1, pieces[s][0])
                    spread_c(g, s)
                    if more or s + 1 < S:
                        spread_b(g, s + 1)
                    if more and s < len(pieces):
                        front(*pieces[s])
                    if s > 0:
                        add_y(g, s - 1)
                    if b + 1 < BANDS:
                        if j in PROJECT_AT:
                            project(f, fb, PROJECT_AT.index(j))
                    elif more:
                        if j == XD_AT:
                            for t in range(TILES):
                                project(f, fb, t)
                        for r in back_at.get(j, ()):
                            back(f, r)
                    if (more or b + 1 < BANDS) and j in DELTA_AT:
                        delta_rows(f, fb, DELTA_AT.index(j))
                add_y(g, S - 1)

            pe.wait_ge(prepared, PREPARED)
            for i, piece in pieces:
                if piece == 0:
                    front_waits(0, i, True)
                front(i, piece)
            for r in range(RUNS):
                back(0, r, True)
            for t in range(TILES):
                project(0, 0, t, True)
            for t in range(TILES):
                delta_rows(0, 0, t)
            spread_b(0, 0, True)
            if last:
                with pe.Fori(0, last) as g:
                    group(g, True)
            group(last, False)


def banded(w, k):
    cols = W + k - 1
    kt = (ROWS + k - 1) // ROWS
    t = np.zeros((C, kt * ROWS, cols, ROWS, W), np.float32)
    for o in range(ROWS):
        for j in range(W):
            t[:, o:o + k, j:j + k, o, j] = w
    t = t.reshape(QUNITS, CQ, kt, ROWS * cols, TOK).transpose(0, 3, 1, 2, 4)
    return np.ascontiguousarray(t)


def lay_out(i):
    def rows(a):
        a = np.tile(a, (GI,) + (1,) * (a.ndim - 1))
        return np.ascontiguousarray(a.reshape((TILES, 128) + a.shape[1:]).swapaxes(0, 1))

    image, channel = np.divmod(np.arange(TILES * 128).reshape(TILES, 128), C)
    xproj = np.zeros((128, TILES, XD), np.float32)
    dtw = np.zeros((XD, TILES, 128), np.float32)
    sel = np.zeros((XD, 2, TILES, 128), np.float32)
    low_rows = np.zeros((XD, 1), np.float32)
    weights = i["L1_conv_x_proj_w"]
    for part in range(2):
        for t in range(TILES):
            for p in range(128):
                m, c = image[t, p], channel[t, p]
                for n in range(N):
                    for k in range(2):
                        row = n * XB + (2 * part + k) * GI + m
                        xproj[p, t, row] = weights[R + k * N + n, c]
                        sel[row, k, t, p] = 1
                        low_rows[row] = part
                dts = m * XB + DT0 + part * R
                xproj[p, t, dts:dts + R] = weights[:R, c]
                dtw[dts:dts + R, t, p] = i["L1_conv_dt_w"][c]
                low_rows[dts:dts + R] = part
    return {
        "x": i["x"], "t1": banded(i["L0_conv_conv_w"][:, 0], K1), "ident": np.eye(128, dtype=np.float32),
        "w1": i["L0_conv_w1"], "w2": i["L0_conv_w2"], "b1": np.ascontiguousarray(i["L0_conv_b1"].reshape(FT, 128).T), "b2": i["L0_conv_b2"],
        "ln_g": i["L0_conv_ln_g"], "ln_b": i["L0_conv_ln_b"], "ls": i["L0_conv_layer_scale"].reshape(C),
        "cb1": i["L0_conv_conv_b"],
        "t2": banded(i["L1_conv_conv_w"][:, 0], K2),
        "xproj": xproj, "dtw": dtw.reshape(XD, -1), "sel": sel.reshape(XD, -1), "low_rows": low_rows,
        "ds": rows(i["L1_conv_Ds"]), "dt_bias": rows(i["L1_conv_dt_b"]), "cb2": rows(i["L1_conv_conv_b"]),
        "a_logs": rows(i["L1_conv_A_logs"]),
    }


def program(nc, groups, a, out):
    x1 = nc.dram_tensor("x1_dram", (IMAGES * C, L), F32, kind="Internal").ap()
    layer0(nc, groups, a["x"], a["t1"], a, x1)
    layer1(nc, groups, x1, a["t2"], a, out)


def kernel(**inputs):
    import concourse.bacc as bacc
    from concourse.bass_utils import run_bass_kernel_spmd

    nc = bacc.Bacc("TRN2", target_bir_lowering=False, num_devices=1)
    arrays = {name: np.ascontiguousarray(a) for name, a in lay_out({k: np.asarray(v) for k, v in inputs.items()}).items()}
    a = {name: nc.dram_tensor(f"in_{name}_dram", v.shape, mybir.dt.from_np(v.dtype), kind="ExternalInput").ap()
         for name, v in arrays.items()}
    out = nc.dram_tensor("out_dram", (IMAGES * C, L), F32, kind="ExternalOutput").ap()
    program(nc, GROUPS, a, out)
    r = run_bass_kernel_spmd(nc, [{f"in_{name}_dram": v for name, v in arrays.items()}], core_ids=[0])
    return r.results[0]["out_dram"].reshape(IMAGES, C, H, W)
```

```python
from contextlib import ExitStack

import numpy as np

import concourse.bass as bass
from concourse import mybir

F32 = mybir.dt.float32
F32R = mybir.dt.float32r
ALU = mybir.AluOpType
ACT = mybir.ActivationFunctionType
AX_X = mybir.AxisListType.X
ds = bass.ds

IMAGES, C, H, W = 32, 96, 56, 56
L = H * W
GI = 4
GROUPS = IMAGES // GI
ROWS = 2
TOK = ROWS * W
IMG_BLK = H // ROWS
BLOCKS = GI * IMG_BLK
BLKS = 4
BT = BLKS * TOK
BANDS = L // BT
UNITS = GI * BANDS
BANK = 512
CQ = 4
QUNITS = C // CQ
TW = 4

K1, PAD1 = 7, 3
COLS1 = W + 2 * PAD1
WIN1 = ROWS * COLS1
KT1 = (ROWS + K1 - 1) // ROWS
NWIN1 = (H + 2 * PAD1) // ROWS
TURNS1 = -(-NWIN1 // TW)
SLOTS1 = 6
FF = 4 * C
FT = FF // 128
FS = 2
LN_EPS = 1e-5
CHUNK = 7
CHUNKS = BLOCKS // CHUNK

K2, PAD2 = 5, 2
COLS2 = W + 2 * PAD2
WIN2 = ROWS * COLS2
KT2 = (ROWS + K2 - 1) // ROWS
NWIN2 = (H + 2 * PAD2) // ROWS
CB = 32
CBS = C // CB
TURNS2 = 2
TW2 = NWIN2 // TURNS2
SLOTS2 = 3
HALVES = 2
SLABS = 3
AHEAD = 5
ZSTEPS = 4
U_SLOTS = 4
U_AHEAD = U_SLOTS - 1
B_AHEAD = U_AHEAD + 1
DA_SLOTS = 4
N, R = 4, 6
EPS = 1e-9
TILES = GI * C // 128
STEPS = TILES * N
XB = 32
DT0 = 4 * GI
XD = N * XB
assert GI == N and DT0 + 2 * R <= XB


def window_copy(win, ps_stage, n):
    i, part = n // TURNS1, n % TURNS1
    a, z = part * TW, min((part + 1) * TW, NWIN1)
    return (win[:, :, i, a:z].rearrange("p c w -> p w c"),
            ps_stage[n % 2][0:WIN1, 0:(z - a) * C].rearrange("p (w c) -> p w c", c=C))


def layer0(nc, groups, x, t1, consts, x1):
    xrow = x.rearrange("b c h w -> (b c) (h w)")
    ximg = x.rearrange("b c h w -> (b c) h w")
    with ExitStack() as ctx:
        def sb(name, shape, dt=F32):
            return ctx.enter_context(nc.sbuf_tensor(name, shape, dt))

        def pb(name):
            return ctx.enter_context(nc.psum_tensor(name, [128, BANK], F32))

        def sem(name):
            return ctx.enter_context(nc.semaphore(name))

        ident = sb("ident1", [128, 128])
        w1 = sb("w1", [C, FF])
        w1_part = [sb(f"w1_{part}", [C, FF], F32R) for part in ("high", "low")]
        w2 = sb("w2", [128, FT, C])
        w2_part = [sb(f"w2_{part}", [128, FS, C], F32R) for part in ("high", "low")]
        b1 = sb("b1", [128, FT])
        b2 = sb("b2", [C, 1])
        gain = sb("gain", [C, 1])
        shift = sb("shift", [C, 1])
        scale_col = sb("scale_col", [C, 1])
        scale_row = sb("scale_row", [128, C])
        bias_row = sb("bias_row", [TOK, C])
        xpad = sb("xpad", [C, H + 2 * PAD1, COLS1])
        win = sb("win", [WIN1, C, GI, NWIN1])
        taps = [sb(f"taps1_{i}", [WIN1, CQ, KT1, TOK]) for i in range(SLOTS1)]
        conv = sb("conv1", [TOK, BLOCKS, C])
        sq = [sb(f"sq{i}", [TOK, CHUNK, C]) for i in range(2)]
        ln_part = sb("ln_part", [TOK, BLOCKS, QUNITS // 2])
        ln_sum = [sb(f"ln_sum{i}", [TOK, CHUNK]) for i in range(2)]
        ln_mean = [sb(f"ln_mean{i}", [TOK, CHUNK]) for i in range(2)]
        ln_ss = [sb(f"ln_ss{i}", [TOK, CHUNK]) for i in range(2)]
        ln_var = [sb(f"ln_var{i}", [TOK, CHUNK]) for i in range(2)]
        ln_rstd = [sb(f"ln_rstd{i}", [TOK, CHUNK]) for i in range(2)]
        minus_half = sb("minus_half", [TOK, CHUNK])
        hn_high = [sb(f"hn_high{i}", [C, BT], F32R) for i in range(2)]
        hn_low = [sb(f"hn_low{i}", [C, BT], F32R) for i in range(2)]
        act_h = [sb(f"act_h{i}", [128, FT, BT]) for i in range(2)]
        h_high = [sb(f"h_high{i}", [128, FS, BT], F32R) for i in range(2)]
        h_low = [sb(f"h_low{i}", [128, FS, BT], F32R) for i in range(2)]
        xres = [sb(f"xres{i}", [C, BT]) for i in range(2)]
        x1o = [sb(f"x1o{i}", [C, BT]) for i in range(2)]

        ps_stage = [pb(f"ps_stage{i}") for i in range(2)]
        ps_back = [pb(f"ps_back{i}") for i in range(2)]
        ps_up = [pb(f"ps_up{i}") for i in range(FT)]
        ps_down = pb("ps_down")

        ident_in = sem("ident_in")
        staged_in = sem("staged_in")
        consts_in = sem("consts_in")
        prepared = sem("prepared")
        xpad_zero = sem("xpad_zero")
        xpad_ready = sem("xpad_ready")
        taps_ready = [sem(f"taps1_ready{i}") for i in range(SLOTS1)]
        xres_ready = [sem(f"xres_ready{i}") for i in range(2)]
        x1_stored = [sem(f"x1_stored{i}") for i in range(2)]
        win_turned = sem("win_turned")
        win_kept_dve = sem("win_kept_dve")
        win_kept_act = sem("win_kept_act")
        conv_done = sem("conv_done")
        conv_kept = sem("conv_kept")
        ln_summed = sem("ln_summed")
        ln_mean_ready = sem("ln_mean_ready")
        ln_centred = sem("ln_centred")
        ln_ss_ready = sem("ln_ss_ready")
        ln_var_ready = sem("ln_var_ready")
        ln_scaled = sem("ln_scaled")
        sq_ready = sem("sq_ready")
        rstd_ready = sem("rstd_ready")
        back_done = sem("back_done")
        hn_high_ready = sem("hn_high_ready")
        hn_ready = sem("hn_ready")
        shift_done = sem("shift_done")
        ln_part_ready = sem("ln_part_ready")
        w1_scaled = sem("w1_scaled")
        w1_high_ready = sem("w1_high_ready")
        up_done = sem("up_done")
        gelu_done = sem("gelu_done")
        h_high_ready = sem("h_high_ready")
        h_low_ready = [sem(f"h_low_ready{t}") for t in range(FS)]
        w2_scaled = sem("w2_scaled")
        w2_high_ready = sem("w2_high_ready")
        down_done = sem("down_done")
        x1_done = sem("x1_done")
        block = ctx.enter_context(nc.Block())

        first_unit = [c * CHUNK // BLKS for c in range(CHUNKS)]
        ln_at = {u: [] for u in range(UNITS)}
        ln_at[-1] = []
        for c in range(2, CHUNKS):
            ln_at[first_unit[c] - 4] += [(c, 0), (c, 1), (c, 2)]
            ln_at[first_unit[c] - 3] += [(c, 3), (c, 4)]
            ln_at[first_unit[c] - 2] += [(c, 5)]
        def staged(k):
            return conv[0:C, :, :].rearrange("p b c -> p (b c)")[:, (k - 1) * L:k * L]

        BORDERS = 4
        TURNS = GI * TURNS1
        TURN = {BANDS * (i - 1) + 3 + k: i * TURNS1 + 2 * k for i in range(1, GI) for k in range(TURNS1 // 2)}

        PREPARED = 5
        last = groups - 1

        @block.sync
        def _(sp):
            c = consts
            loads = [(ident[:, :], c["ident"]), (w1[:, :], c["w1"]),
                     (w2[:, :, :], c["w2"].rearrange("(t p) c -> p t c", p=128)),
                     (b1[:, :], c["b1"]),
                     (b2[:, :], c["b2"].rearrange("(p o) -> p o", o=1)),
                     (gain[:, :], c["ln_g"].rearrange("(p o) -> p o", o=1)),
                     (shift[:, :], c["ln_b"].rearrange("(p o) -> p o", o=1)),
                     (scale_col[:, :], c["ls"].rearrange("(p o) -> p o", o=1)),
                     (scale_row[:, :], c["ls"].partition_broadcast(128)),
                     (bias_row[:, :], c["cb1"].partition_broadcast(TOK))]
            def load_image(f, i):
                sp.dma_start(xpad[:, PAD1:PAD1 + H, PAD1:PAD1 + W],
                             ximg[ds((f * GI + i) * C, C), :, :]).then_inc(xpad_ready, 16)

            def load_taps(q):
                slot = q % SLOTS1
                sp.dma_start(taps[slot][:, :, :, :], t1[q]).then_inc(taps_ready[slot], 16)

            def load_xres(f, u):
                sp.dma_start(xres[u % 2][:, :],
                             xrow[ds((f * GI + u // BANDS) * C, C), (u % BANDS) * BT:(u % BANDS + 1) * BT]
                             ).then_inc(xres_ready[u % 2], 16)

            sp.dma_start(*loads[0]).then_inc(ident_in, 16)
            sp.wait_ge(xpad_zero, BORDERS)
            load_image(0, 0)
            for k in range(1, GI):
                sp.dma_start(staged(k), xrow[k * C:(k + 1) * C, :]).then_inc(staged_in, 16)
            load_taps(0)
            for dst, src in loads[1:]:
                sp.dma_start(dst, src).then_inc(consts_in, 16)
            for q in range(1, SLOTS1):
                load_taps(q)
            load_xres(0, 0)
            load_xres(0, 1)

            def group(g, more):
                if more:
                    sp.wait_ge(win_turned, (g + 1) * TURNS)
                    load_image(g + 1, 0)
                for q in range(QUNITS):
                    if more or q + SLOTS1 < QUNITS:
                        sp.wait_ge(conv_done, g * QUNITS + q + 1)
                        load_taps((q + SLOTS1) % QUNITS)
                for u in range(UNITS):
                    if more and (u == 0 or u % BANDS == BANDS - 1) and (u + 1) // BANDS + 1 < GI:
                        i = (u + 1) // BANDS + 1
                        sp.wait_ge(win_turned, (g + 1) * TURNS + TURNS1 * i)
                        load_image(g + 1, i)
                    sp.wait_ge(x1_done, g * UNITS + u + 1)
                    sp.dma_start(x1[ds((g * GI + u // BANDS) * C, C), (u % BANDS) * BT:(u % BANDS + 1) * BT],
                                 x1o[u % 2][:, :]).then_inc(x1_stored[u % 2], 16)
                    if u + 2 < UNITS:
                        load_xres(g, u + 2)
                    elif more:
                        load_xres(g + 1, u + 2 - UNITS)

            if last:
                with sp.Fori(0, last) as g:
                    group(g, True)
            group(last, False)
            for p in range(2):
                sp.wait_ge(x1_stored[p], 16 * (groups * UNITS // 2 + 1))

        @block.gpsimd
        def _(pool):
            nc.gpsimd.memset(minus_half[:, :], -0.5).then_inc(prepared, 1)
            pool.sem_inc(x1_stored[0], 16)
            pool.sem_inc(x1_stored[1], 16)
            pool.wait_ge(prepared, PREPARED)

            def rstd(g, c):
                pool.wait_ge(ln_var_ready, g * CHUNKS + c + 1)
                nc.gpsimd.tensor_tensor(ln_rstd[c % 2][:, :], ln_var[c % 2][:, :], minus_half[:, :],
                                        ALU.pow).then_inc(rstd_ready, 1)

            def h_low_part(g, u):
                pool.wait_ge(h_high_ready, (g * UNITS + u) * FS + 2)
                nc.gpsimd.tensor_tensor(h_low[u % 2][:, 1, :], act_h[u % 2][:, 1, :], h_high[u % 2][:, 1, :],
                                        ALU.subtract).then_inc(h_low_ready[1], 1)

            def group(g):
                rstd(g, 0)
                rstd(g, 1)
                for u in range(UNITS):
                    h_low_part(g, u)
                    for c, step in ln_at[u]:
                        if step == 4:
                            rstd(g, c)

            with pool.Fori(0, groups) as g:
                group(g)

        @block.vector
        def _(dve):
            for border in (xpad[:, 0:PAD1, :], xpad[:, PAD1 + H:, :],
                           xpad[:, PAD1:PAD1 + H, 0:PAD1], xpad[:, PAD1:PAD1 + H, PAD1 + W:]):
                nc.vector.memset(border, 0.0).then_inc(xpad_zero, 1)

            def split_weights():
                dve.wait_ge(consts_in, 16 * 9)
                dve.wait_ge(shift_done, 1)
                nc.vector.tensor_tensor(b1[:, :], b1[:, :], ps_down[:, 0:FT], ALU.add).then_inc(prepared, 1)
                nc.vector.tensor_scalar(w1[:, :], w1[:, :], gain[:, 0:1], None, ALU.mult).then_inc(w1_scaled, 1)
                dve.wait_ge(w1_scaled, 1)
                nc.vector.tensor_copy(w1_part[0][:, :], w1[:, :]).then_inc(w1_high_ready, 1)
                dve.wait_ge(w1_high_ready, 1)
                nc.vector.tensor_tensor(w1_part[1][:, :], w1[:, :], w1_part[0][:, :], ALU.subtract).then_inc(prepared, 1)
                nc.vector.tensor_tensor(w2[:, :, :], w2[:, :, :],
                                        scale_row[:, :].unsqueeze(1).broadcast_to([128, FT, C]),
                                        ALU.mult).then_inc(w2_scaled, 1)
                nc.vector.tensor_tensor(b2[:, :], b2[:, :], scale_col[:, :], ALU.mult).then_inc(prepared, 1)
                dve.wait_ge(w2_scaled, 1)
                nc.vector.tensor_copy(w2_part[0][:, :, :], w2[:, 0:FS, :]).then_inc(w2_high_ready, 1)
                dve.wait_ge(w2_high_ready, 1)
                nc.vector.tensor_tensor(w2_part[1][:, :, :], w2[:, 0:FS, :], w2_part[0][:, :, :],
                                        ALU.subtract).then_inc(prepared, 1)

            def keep_windows(f, n):
                dve.wait_ge(win_turned, f * TURNS + n + 1)
                nc.vector.tensor_copy(*window_copy(win, ps_stage, n)).then_inc(win_kept_dve, 1)

            def channel_sums(g, k):
                dve.wait_ge(conv_kept, g * QUNITS + 2 * k + 2)
                nc.vector.tensor_reduce(ln_part[:, :, k], conv[:, :, 2 * k * CQ:(2 * k + 2) * CQ], AX_X,
                                        ALU.add).then_inc(ln_part_ready, 1)

            def ln(g, c, step):
                n = g * CHUNKS + c + 1
                blocks = conv[:, c * CHUNK:(c + 1) * CHUNK, :]
                wide = [TOK, CHUNK, C]
                k = c % 2
                if step == 0:
                    nc.vector.tensor_reduce(ln_sum[k][:, :], ln_part[:, c * CHUNK:(c + 1) * CHUNK, :], AX_X,
                                            ALU.add).then_inc(ln_summed, 1)
                elif step == 1:
                    dve.wait_ge(ln_summed, n)
                    nc.vector.tensor_scalar(ln_mean[k][:, :], ln_sum[k][:, :], 1.0 / C, None,
                                            ALU.mult).then_inc(ln_mean_ready, 1)
                elif step == 2:
                    dve.wait_ge(ln_mean_ready, n)
                    nc.vector.tensor_tensor(blocks, blocks, ln_mean[k][:, :].unsqueeze(2).broadcast_to(wide),
                                            ALU.subtract).then_inc(ln_centred, 1)
                elif step == 3:
                    dve.wait_ge(sq_ready, n)
                    nc.vector.tensor_reduce(ln_ss[k][:, :], sq[k][:, :, :], AX_X, ALU.add).then_inc(ln_ss_ready, 1)
                elif step == 4:
                    dve.wait_ge(ln_ss_ready, n)
                    nc.vector.tensor_scalar(ln_var[k][:, :], ln_ss[k][:, :], 1.0 / C, LN_EPS, ALU.mult,
                                            ALU.add).then_inc(ln_var_ready, 1)
                else:
                    dve.wait_ge(rstd_ready, n)
                    nc.vector.tensor_tensor(blocks, blocks, ln_rstd[k][:, :].unsqueeze(2).broadcast_to(wide),
                                            ALU.mult).then_inc(ln_scaled, 1)

            def normed(g, u):
                dve.wait_ge(hn_high_ready, g * UNITS + u + 1)
                nc.vector.tensor_tensor(hn_low[u % 2][:, :], ps_back[u % 2][0:C, 0:BT], hn_high[u % 2][:, :],
                                        ALU.subtract).then_inc(hn_ready, 1)

            def residual(g, u):
                dve.wait_ge(down_done, g * UNITS + u + 1)
                dve.wait_ge(xres_ready[u % 2], (g * (UNITS // 2) + u // 2 + 1) * 16)
                dve.wait_ge(x1_stored[u % 2], (g * (UNITS // 2) + u // 2 + 1) * 16)
                nc.vector.scalar_tensor_tensor(x1o[u % 2][:, :], ps_down[0:C, 0:BT], b2[:, 0:1],
                                               xres[u % 2][:, :], ALU.add, ALU.add).then_inc(x1_done, 1)

            def h_low_part(g, u):
                dve.wait_ge(h_high_ready, (g * UNITS + u) * FS + 1)
                nc.vector.tensor_tensor(h_low[u % 2][:, 0, :], act_h[u % 2][:, 0, :], h_high[u % 2][:, 0, :],
                                        ALU.subtract).then_inc(h_low_ready[0], 1)

            def group(g, more):
                for q in range(QUNITS):
                    dve.wait_ge(conv_done, g * QUNITS + q + 1)
                    nc.vector.tensor_tensor(
                        conv[:, :, q * CQ:(q + 1) * CQ].rearrange("p b c -> p c b"),
                        ps_stage[q % 2][0:TOK, 0:CQ * BLOCKS].rearrange("p (c b) -> p c b", c=CQ),
                        bias_row[:, q * CQ:(q + 1) * CQ].unsqueeze(2).broadcast_to([TOK, CQ, BLOCKS]),
                        ALU.add).then_inc(conv_kept, 1)
                    if q > 0 and q % 2 == 0:
                        channel_sums(g, q // 2 - 1)
                channel_sums(g, QUNITS // 2 - 1)
                dve.wait_ge(ln_part_ready, (g + 1) * (QUNITS // 2))
                for c, step in ((0, 0), (0, 1), (1, 0), (0, 2), (1, 1), ("windows", 0), (0, 3), (0, 4), (1, 2),
                                ("windows", 2), (0, 5), ("normed", 0), ("windows", 4), (1, 3), (1, 4), (2, 0), (2, 1),
                                (1, 5), ("windows", 6), (2, 2)):
                    if c == "normed":
                        normed(g, 0)
                    elif c != "windows":
                        ln(g, c, step)
                    elif more:
                        keep_windows(g + 1, step)
                for u in range(UNITS):
                    if u + 1 < UNITS:
                        normed(g, u + 1)
                    if more and u in TURN:
                        keep_windows(g + 1, TURN[u])
                    for c, step in ln_at[u]:
                        if step in (0, 1, 5):
                            ln(g, c, step)
                    if u > 0:
                        residual(g, u - 1)
                    for c, step in ln_at[u]:
                        if step in (2, 3, 4):
                            ln(g, c, step)
                    h_low_part(g, u)
                residual(g, UNITS - 1)

            for n in range(0, TURNS, 2):
                keep_windows(0, n)
                k = n // TURNS1 + 1
                if n == k * TURNS1 - 2 and k < GI:
                    dve.wait_ge(staged_in, 16 * (GI - 1))
                    dve.wait_ge(win_turned, k * TURNS1)
                    nc.vector.tensor_copy(xpad[:, PAD1:PAD1 + H, PAD1:PAD1 + W],
                                          staged(k).rearrange("p (h w) -> p h w", h=H)).then_inc(xpad_ready, 16)
            split_weights()
            if last:
                with dve.Fori(0, last) as g:
                    group(g, True)
            group(last, False)

        @block.scalar
        def _(act):
            def keep_windows(f, n):
                act.wait_ge(win_turned, f * TURNS + n + 1)
                nc.scalar.activation(*window_copy(win, ps_stage, n), ACT.Copy).then_inc(win_kept_act, 1)

            def square(g, c):
                act.wait_ge(ln_centred, g * CHUNKS + c + 1)
                nc.scalar.activation(sq[c % 2][:, :, :], conv[:, c * CHUNK:(c + 1) * CHUNK, :],
                                     ACT.Square).then_inc(sq_ready, 1)

            def hn_high_part(g, u):
                act.wait_ge(back_done, g * UNITS + u + 1)
                nc.scalar.activation(hn_high[u % 2][:, :], ps_back[u % 2][0:C, 0:BT],
                                     ACT.Copy).then_inc(hn_high_ready, 1)

            def gelu(g, u):
                if u >= 2:
                    act.wait_ge(down_done, g * UNITS + u - 1)
                for t in range(FT):
                    act.wait_ge(up_done, (g * UNITS + u) * FT + t + 1)
                    nc.scalar.activation(act_h[u % 2][:, t, :], ps_up[t][:, 0:BT], ACT.Gelu,
                                         bias=b1[:, t:t + 1]).then_inc(gelu_done, 1)

            def h_high_part(g, u, t):
                act.wait_ge(gelu_done, (g * UNITS + u) * FT + t + 1)
                nc.scalar.activation(h_high[u % 2][:, t, :], act_h[u % 2][:, t, :], ACT.Copy).then_inc(h_high_ready, 1)

            def group(g, more):
                act.preload_act_table_set("gelu_and_others")
                if more:
                    keep_windows(g + 1, 1)
                square(g, 0)
                if more:
                    keep_windows(g + 1, 3)
                square(g, 1)
                hn_high_part(g, 0)
                if more:
                    keep_windows(g + 1, 5)
                for u in range(UNITS):
                    gelu(g, u)
                    if more and u == 0:
                        keep_windows(g + 1, 7)
                    if u + 1 < UNITS:
                        hn_high_part(g, u + 1)
                    for t in range(FS):
                        h_high_part(g, u, t)
                    if more and u in TURN:
                        keep_windows(g + 1, TURN[u] + 1)
                    for c in range(2, CHUNKS):
                        if first_unit[c] - 3 == u:
                            square(g, c)

            for n in range(1, TURNS, 2):
                keep_windows(0, n)
            act.wait_ge(prepared, PREPARED)
            if last:
                with act.Fori(0, last) as g:
                    group(g, True)
            group(last, False)

        @block.tensor
        def _(pe):
            def turn_windows(f, first, n):
                i, part = n // TURNS1, n % TURNS1
                if part == 0:
                    pe.wait_ge(xpad_ready, (f * GI + i + 1) * 16)
                if n >= 2:
                    pe.wait_ge((win_kept_dve, win_kept_act)[n % 2], f * (TURNS // 2) + n // 2)
                elif not first:
                    pe.wait_ge(conv_kept, f * QUNITS)
                pixels = xpad[:, :, :].rearrange("p r w -> p (r w)")
                for j, w in enumerate(range(part * TW, min((part + 1) * TW, NWIN1))):
                    mm = nc.tensor.transpose(ps_stage[n % 2][0:WIN1, j * C:(j + 1) * C],
                                             pixels[:, w * WIN1:(w + 1) * WIN1], ident[0:C, 0:C])
                mm.then_inc(win_turned, 1)

            def convolve(g):
                pe.wait_ge(win_kept_dve, (g + 1) * (TURNS // 2))
                pe.wait_ge(win_kept_act, (g + 1) * (TURNS // 2))
                for q in range(QUNITS):
                    pe.wait_ge(taps_ready[q % SLOTS1], (g * (QUNITS // SLOTS1) + q // SLOTS1 + 1) * 16)
                    if q >= 2:
                        pe.wait_ge(conv_kept, g * QUNITS + q - 1)
                    for c in range(CQ):
                        for k in range(KT1):
                            mm = nc.tensor.matmul(
                                ps_stage[q % 2][0:TOK, c * BLOCKS:(c + 1) * BLOCKS],
                                taps[q % SLOTS1][:, c, k, :],
                                win[:, q * CQ + c, :, k:k + IMG_BLK],
                                start=(k == 0), stop=(k == KT1 - 1))
                    mm.then_inc(conv_done, 1)

            def back(g, u):
                pe.wait_ge(ln_scaled, g * CHUNKS + (u * BLKS + BLKS - 1) // CHUNK + 1)
                if u >= 2:
                    pe.wait_ge(hn_ready, g * UNITS + u - 1)
                for j in range(BLKS):
                    mm = nc.tensor.transpose(ps_back[u % 2][0:C, j * TOK:(j + 1) * TOK],
                                             conv[:, u * BLKS + j, :], ident[0:TOK, 0:TOK])
                mm.then_inc(back_done, 1)

            def up(g, u):
                pe.wait_ge(hn_ready, g * UNITS + u + 1)
                for t in range(FT):
                    if u > 0:
                        pe.wait_ge(gelu_done, (g * UNITS + u - 1) * FT + t + 1)
                    cols = slice(t * 128, (t + 1) * 128)
                    nc.tensor.matmul(ps_up[t][:, 0:BT], w1_part[0][:, cols], hn_high[u % 2][:, :],
                                     start=True, stop=False)
                    nc.tensor.matmul(ps_up[t][:, 0:BT], w1_part[1][:, cols], hn_high[u % 2][:, :],
                                     start=False, stop=False)
                    nc.tensor.matmul(ps_up[t][:, 0:BT], w1_part[0][:, cols], hn_low[u % 2][:, :],
                                     start=False, stop=True).then_inc(up_done, 1)

            def down(g, u):
                pe.wait_ge(gelu_done, (g * UNITS + u + 1) * FT)
                if u > 0:
                    pe.wait_ge(x1_done, g * UNITS + u)
                for t in range(FS, FT):
                    nc.tensor.matmul(ps_down[0:C, 0:BT], w2[:, t, :], act_h[u % 2][:, t, :],
                                     start=(t == FS), stop=False)
                for t in range(FS):
                    pe.wait_ge(h_low_ready[t], g * UNITS + u + 1)
                    high, low = h_high[u % 2][:, t, :], h_low[u % 2][:, t, :]
                    nc.tensor.matmul(ps_down[0:C, 0:BT], w2_part[0][:, t, :], high, start=False, stop=False)
                    nc.tensor.matmul(ps_down[0:C, 0:BT], w2_part[1][:, t, :], high, start=False, stop=False)
                    mm = nc.tensor.matmul(ps_down[0:C, 0:BT], w2_part[0][:, t, :], low,
                                          start=False, stop=(t == FS - 1))
                mm.then_inc(down_done, 1)

            def group(g, more):
                convolve(g)
                if more:
                    for n in range(4):
                        turn_windows(g + 1, False, n)
                back(g, 0)
                if more:
                    for n in (4, 5):
                        turn_windows(g + 1, False, n)
                for u in range(UNITS):
                    up(g, u)
                    if more and u == 0:
                        for n in (6, 7):
                            turn_windows(g + 1, False, n)
                    if u + 1 < UNITS:
                        back(g, u + 1)
                    if more and u in TURN:
                        turn_windows(g + 1, False, TURN[u])
                        turn_windows(g + 1, False, TURN[u] + 1)
                    if u > 0:
                        down(g, u - 1)
                down(g, UNITS - 1)

            pe.wait_ge(ident_in, 16)
            for n in range(TURNS):
                turn_windows(0, True, n)
            pe.wait_ge(consts_in, 16 * 9)
            for t in range(FT):
                mm = nc.tensor.matmul(ps_down[:, t:t + 1], w1[:, t * 128:(t + 1) * 128], shift[:, 0:1],
                                      start=True, stop=True)
            mm.then_inc(shift_done, 1)
            pe.wait_ge(prepared, PREPARED)
            if last:
                with pe.Fori(0, last) as g:
                    group(g, True)
            group(last, False)


def layer1(nc, groups, x1, t2, consts, out):
    x1img = x1.rearrange("r (h w) -> r h w", h=H)
    with ExitStack() as ctx:
        def sb(name, shape, dt=F32):
            return ctx.enter_context(nc.sbuf_tensor(name, shape, dt))

        def pb(name):
            return ctx.enter_context(nc.psum_tensor(name, [128, BANK], F32))

        def sem(name):
            return ctx.enter_context(nc.semaphore(name))

        ident = sb("ident2", [128, 128])
        xproj = sb("xproj", [128, TILES, XD])
        dtw = [sb(f"dtw_{part}", [XD, TILES, 128], F32R) for part in ("high", "low")]
        sel = sb("sel", [XD, 2, TILES, 128], F32R)
        low_rows = sb("low_rows", [XD, 1])
        skip = sb("skip", [128, TILES, 128])
        ds_col = sb("ds_col", [128, TILES])
        dt_bias = sb("dt_bias", [128, TILES])
        conv_bias = sb("conv_bias", [128, TILES])
        a_neg = sb("a_neg", [128, TILES, N])
        zeros = sb("zeros", [128, STEPS])
        q_first = sb("q_first", [128, STEPS])
        xpad = sb("x1pad", [C, H + 2 * PAD2, COLS2])
        win = [sb(f"win2_{i}", [WIN2, CB, GI, NWIN2]) for i in range(2)]
        taps = [sb(f"taps2_{i}", [WIN2, CQ, KT2, TOK]) for i in range(SLOTS2)]
        conv = sb("conv2", [TOK, IMG_BLK, GI * C])
        xs = sb("xs", [128, TILES, L])
        xd = sb("xd", [XD, BT])
        high = sb("high", [XD, BT], F32R)
        parts = [sb(f"parts{i}", [XD, BT], F32R) for i in range(3)]
        z_pos = sb("z_pos", [128, TILES, BT])
        z_log = sb("z_log", [128, TILES, BT])
        delta = sb("delta", [128, TILES, BT])
        dxs = sb("dxs", [128, TILES, BT])
        d_a = [sb(f"d_a{i}", [128, BT]) for i in range(DA_SLOTS)]
        q = [sb(f"q{i}", [128, BT]) for i in range(2)]
        b_rows = [sb(f"b_rows{i}", [128, BT]) for i in range(2)]
        u = [sb(f"u{i}", [128, BT]) for i in range(U_SLOTS)]
        hc = [sb(f"hc{i}", [128, BT]) for i in range(2)]
        q_last = sb("q_last", [128, STEPS])
        h_last = sb("h_last", [128, STEPS])
        y = [sb(f"y{i}", [128, BT]) for i in range(2)]

        ps_front = [pb(f"ps_front{i}") for i in range(2)]
        ps_prep = [pb(f"ps_prep{i}") for i in range(2)]
        ps_b = [pb(f"ps_b{i}") for i in range(2)]
        ps_c = pb("ps_c")
        ps_y = pb("ps_y")

        consts_in = sem("consts2_in")
        prepared = sem("prepared2")
        slab_ready = [sem(f"slab_ready{i}") for i in range(SLABS)]
        taps_ready = [sem(f"taps2_ready{i}") for i in range(SLOTS2)]
        front_done = sem("front_done")
        front_kept = sem("front_kept")
        back_done = sem("back2_done")
        xs_kept = sem("xs_kept")
        xd_done = sem("xd_done")
        xd_ready = sem("xd_ready")
        parts_ready = sem("parts_ready")
        z_done = sem("z_done")
        dtw_high = sem("dtw_high")
        a_ready = sem("a_ready")
        ident_in = sem("ident2_in")
        xpad_zero = sem("x1pad_zero")
        z_step = sem("z_step")
        delta_ready = sem("delta_ready")
        dxs_ready = sem("dxs_ready")
        d_a_ready = sem("d_a_ready")
        b_ready = sem("b_ready")
        c_ready = sem("c_ready")
        clamp_done = sem("clamp_done")
        q_done = sem("q_done")
        u_done = sem("u_done")
        gated = sem("gated")
        b_kept = sem("b_kept")
        h_done = sem("h_done")
        hc_done = sem("hc_done")
        q_kept = sem("q_kept")
        h_kept = sem("h_kept")
        y_done = sem("y_done")
        y_kept = sem("y_kept")
        y_stored = [sem(f"y_stored{i}") for i in range(2)]
        block = ctx.enter_context(nc.Block())

        last = groups - 1
        CONSTS = 16 * 8
        BORDERS = 4
        PREPARED = 2 + TILES + 3
        S = BANDS * STEPS
        RUNS = BANDS * TILES
        FRONT = CBS * (GI * TURNS2 + CB // CQ)
        turns = [[("turn", cb, i, p) for i in range(GI) for p in range(TURNS2)] for cb in range(CBS)]
        units = list(turns[0])
        assert len(turns[0]) == CB // CQ
        for cb in range(CBS):
            for cu in range(CB // CQ):
                units.append(("conv", cb, cu, 0))
                if cb + 1 < CBS:
                    units.append(turns[cb + 1][cu])
        pieces = [(i, piece) for i in range(FRONT) for piece in range(1 if units[i][0] == "turn" else HALVES)]
        assert len(pieces) <= S - STEPS
        last_piece = {i: s for s, (i, _) in enumerate(pieces)}
        step_of = [s for s, (i, piece) in enumerate(pieces) if piece == 0]
        turn_unit = [units.index(("turn", k // GI, k % GI, TURNS2 - 1)) for k in range(CBS * GI)]
        conv_unit = [units.index(("conv", k // (CB // CQ), k % (CB // CQ), 0)) for k in range(QUNITS)]

        back_at = {0: range(0, TILES), 8: range(TILES, TILES + 4), 9: range(TILES + 4, 12), 11: range(12, RUNS)}
        silu_at = {0: (0, TILES), 9: (TILES, 12), 11: (12, RUNS)}
        back_banks = ps_prep + ps_front

        PROJECT_AT = (0, 1, 2)
        XD_AT = 3
        SPLIT_AT = 4
        DELTA_AT = [(4, 6, 8)] * (BANDS - 1) + [(4, 5, 6)]
        Z_AT = [(5, 7, 9)] * (BANDS - 1) + [(5, 6, 7)]
        SUM_AT = (7, 9, 11)

        def parts_slot(b):
            return 2 if b == 0 else b % 2

        def next_band(g, b):
            return (g, b + 1) if b + 1 < BANDS else (g + 1, 0)

        @block.sync
        def _(sp):
            sp.dma_start(ident[:, :], consts["ident"]).then_inc(ident_in, 16)
            small = [(xproj[:, :, :], consts["xproj"]),
                     (xs[:, 0, 0:2 * TILES * 128], consts["sel"]),
                     (xs[:, 1, 0:TILES * 128], consts["dtw"]),
                     (ds_col[:, :], consts["ds"]), (dt_bias[:, :], consts["dt_bias"]),
                     (conv_bias[:, :], consts["cb2"]), (low_rows[:, :], consts["low_rows"]),
                     (a_neg[:, :, :], consts["a_logs"])]

            def load_slab(f, first, k):
                if k >= SLABS:
                    sp.wait_ge(front_done, f * FRONT + turn_unit[k - SLABS] + 1)
                elif not first:
                    sp.wait_ge(front_done, (f - 1) * FRONT + turn_unit[k - SLABS] + 1)
                rows = slice(CB * (k % SLABS), CB * (k % SLABS) + CB)
                sp.dma_start(xpad[rows, PAD2:PAD2 + H, PAD2:PAD2 + W],
                             x1img[ds((f * GI + k % GI) * C + CB * (k // GI), CB), :, :]
                             ).then_inc(slab_ready[k % SLABS], 16)

            def load_taps(f, first, k):
                if k >= SLOTS2:
                    sp.wait_ge(front_done, f * FRONT + conv_unit[k - SLOTS2] + 1)
                elif not first:
                    sp.wait_ge(front_done, (f - 1) * FRONT + conv_unit[k - SLOTS2] + 1)
                sp.dma_start(taps[k % SLOTS2][:, :, :, :], t2[k]).then_inc(taps_ready[k % SLOTS2], 16)

            loads = [(load_slab, k, turn_unit[k] - TURNS2 + 1) for k in range(CBS * GI)]
            loads += [(load_taps, k, conv_unit[k]) for k in range(QUNITS)]
            loads.sort(key=lambda load: load[2])

            sp.wait_ge(xpad_zero, BORDERS)
            for n, (load, k, _) in enumerate(loads):
                if n == SLABS:
                    for dst, src in small:
                        sp.dma_start(dst, src).then_inc(consts_in, 16)
                load(0, True, k)

            def store(g, r):
                b, t = r // TILES, r % TILES
                sp.wait_ge(y_kept, g * RUNS + r + 2)
                sp.dma_start(out[ds(g * GI * C + t * 128, 128), b * BT:(b + 1) * BT],
                             y[r % 2][:, :]).then_inc(y_stored[r % 2], 16)

            def first_slabs(f):
                for load, k, _ in loads[:SLABS]:
                    load(f, False, k)

            def group(g, ahead):
                todo = loads[SLABS:] if ahead else []
                for s in range(S):
                    if ahead == 2 and s == S - 2 * STEPS:
                        first_slabs(g + 2)
                    while todo and step_of[todo[0][2]] <= s + AHEAD:
                        load, k, _ = todo.pop(0)
                        load(g + 1, False, k)
                    if s >= N + 2 and (s - N - 2) % N == 0:
                        store(g, (s - N - 2) // N)
                store(g, RUNS - 1)

            if last:
                first_slabs(1)
            if last > 1:
                with sp.Fori(0, last - 1) as g:
                    group(g, 2)
            if last:
                group(last - 1, 1)
            group(last, 0)
            for p in range(2):
                sp.wait_ge(y_stored[p], (groups * ((RUNS + 1 - p) // 2) + 1) * 16)

        @block.gpsimd
        def _(pool):
            nc.gpsimd.memset(zeros[:, :], 0.0).then_inc(prepared, 1)
            nc.gpsimd.memset(q_first[:, :], float(np.float32(1) / np.float32(EPS))).then_inc(prepared, 1)
            pool.sem_inc(y_stored[0], 16)
            pool.sem_inc(y_stored[1], 16)
            pool.sem_inc(y_kept, 1)
            pool.sem_inc(h_done, 1)
            pool.wait_ge(prepared, PREPARED)

            def add(o, a, b):
                return nc.gpsimd.tensor_tensor(o, a, b, ALU.add)

            def split(f, b):
                pool.wait_ge(xd_ready, (f * BANDS + b + 1) * 2)
                nc.gpsimd.tensor_tensor(parts[parts_slot(b)][:, :], xd[:, :], high[:, :],
                                        ALU.subtract).then_inc(parts_ready, 1)

            def sum_delta(f, b, t, first=False):
                pool.wait_ge(z_step, (f * RUNS + b * TILES + t + 1) * ZSTEPS)
                if not first:
                    pool.wait_ge(d_a_ready, (f * BANDS + b - 1) * STEPS + (t + 1) * N)
                    pool.wait_ge(u_done, (f * BANDS + b - 1) * STEPS + (t + 1) * N)
                add(delta[:, t, :], z_pos[:, t, :], z_log[:, t, :]).then_inc(delta_ready, 1)

            def times_x(f, b, t):
                pool.wait_ge(delta_ready, f * RUNS + b * TILES + t + 1)
                nc.gpsimd.tensor_tensor(dxs[:, t, :], delta[:, t, :], xs[:, t, b * BT:(b + 1) * BT],
                                        ALU.mult).then_inc(dxs_ready, 1)

            def times_b(g, s):
                pool.wait_ge(b_kept, g * S + s + 1)
                pool.wait_ge(h_kept, g * S + s - U_SLOTS + 1 + STEPS)
                if s % N == 0:
                    pool.wait_ge(dxs_ready, g * RUNS + s // N + 1)
                nc.gpsimd.tensor_tensor(u[s % U_SLOTS][:, :], dxs[:, s % STEPS // N, :], b_rows[s % 2][:, :],
                                        ALU.mult).then_inc(u_done, 1)

            def group(g, more):
                for s in range(S):
                    b, j = s // STEPS, s % STEPS
                    f, fb = next_band(g, b)
                    prepare = more or b + 1 < BANDS
                    pool.wait_ge(q_done, g * S + s + 1)
                    q_from = q[s % 2][:, BT - 1:BT] if b + 1 < BANDS else q_first[:, 0:1]
                    add(q_last[:, j:j + 1], q_from, zeros[:, 0:1]).then_inc(q_kept, 1)
                    if prepare and j == SPLIT_AT:
                        split(f, fb)
                    if prepare and j in SUM_AT:
                        sum_delta(f, fb, SUM_AT.index(j))
                    if prepare and j - 1 in SUM_AT:
                        times_x(f, fb, SUM_AT.index(j - 1))
                    pool.wait_ge(h_done, g * S + s + 2)
                    h_from = u[s % U_SLOTS][:, BT - 1:BT] if b + 1 < BANDS else zeros[:, 0:1]
                    add(h_last[:, j:j + 1], h_from, zeros[:, 0:1]).then_inc(h_kept, 1)
                    if more or s + U_AHEAD < S:
                        times_b(g, s + U_AHEAD)
                    if prepare and j == STEPS - 1:
                        times_x(f, fb, TILES - 1)

            add(q_last[:, :], q_first[:, :], zeros[:, :]).then_inc(q_kept, STEPS)
            add(h_last[:, :], zeros[:, :], zeros[:, :]).then_inc(h_kept, STEPS)
            split(0, 0)
            for t in range(TILES):
                sum_delta(0, 0, t, True)
                times_x(0, 0, t)
            for s in range(U_AHEAD):
                times_b(0, s)
            if last:
                with pool.Fori(0, last) as g:
                    group(g, True)
            group(last, False)

        @block.vector
        def _(dve):
            for border in (xpad[:, 0:PAD2, :], xpad[:, PAD2 + H:, :],
                           xpad[:, PAD2:PAD2 + H, 0:PAD2], xpad[:, PAD2:PAD2 + H, PAD2 + W:]):
                nc.vector.memset(border, 0.0).then_inc(xpad_zero, 1)
            dve.wait_ge(consts_in, CONSTS)
            staged = xs[:, 1, 0:TILES * 128].rearrange("p (t q) -> p t q", t=TILES)
            nc.vector.tensor_copy(sel[:, :, :, :].rearrange("p k t q -> p (k t q)"),
                                  xs[:, 0, 0:2 * TILES * 128]).then_inc(prepared, 1)
            nc.vector.tensor_copy(dtw[0][:, :, :], staged).then_inc(dtw_high, 1)
            for t in range(TILES):
                nc.vector.tensor_scalar(skip[:, t, :], ident[:, :], ds_col[:, t:t + 1], None,
                                        ALU.mult).then_inc(prepared, 1)
            dve.wait_ge(dtw_high, 1)
            nc.vector.tensor_tensor(dtw[1][:, :, :], staged, dtw[0][:, :, :], ALU.subtract).then_inc(prepared, 1)
            dve.wait_ge(a_ready, 1)
            nc.vector.tensor_scalar(a_neg[:, :, :], a_neg[:, :, :], -1.0, None, ALU.mult).then_inc(prepared, 1)

            def clamp(g, s):
                dve.wait_ge(d_a_ready, g * S + s + 1)
                nc.vector.tensor_scalar(d_a[s % DA_SLOTS][:, :], d_a[s % DA_SLOTS][:, :], float(np.float32(EPS)), None,
                                        ALU.max).then_inc(clamp_done, 1)

            def scan_q(g, s):
                j = s % STEPS
                dve.wait_ge(clamp_done, g * S + s + 1)
                dve.wait_ge(q_kept, g * S + s + STEPS - 1)
                nc.vector.tensor_tensor_scan(q[s % 2][:, :], d_a[s % DA_SLOTS][:, :],
                                             zeros[:, 0:1].broadcast_to([128, BT]), q_last[:, j:j + 1],
                                             ALU.mult, ALU.add).then_inc(q_done, 1)

            def gate(g, s):
                dve.wait_ge(q_done, g * S + s + 1)
                dve.wait_ge(u_done, g * S + s + 1)
                nc.vector.scalar_tensor_tensor(u[s % U_SLOTS][:, :], q[s % 2][:, :], 1.0, u[s % U_SLOTS][:, :],
                                               ALU.min, ALU.mult).then_inc(gated, 1)

            def scan_h(g, s):
                j = s % STEPS
                dve.wait_ge(gated, g * S + s + 1)
                dve.wait_ge(h_kept, g * S + s + STEPS - 1)
                nc.vector.tensor_tensor_scan(u[s % U_SLOTS][:, :], d_a[s % DA_SLOTS][:, :], u[s % U_SLOTS][:, :], h_last[:, j:j + 1],
                                             ALU.mult, ALU.add).then_inc(h_done, 1)

            def times_c(g, s):
                dve.wait_ge(h_done, g * S + s + 2)
                dve.wait_ge(c_ready, g * S + s + 1)
                nc.vector.tensor_tensor(hc[s % 2][:, :], u[s % U_SLOTS][:, :], ps_c[:, 0:BT], ALU.mult).then_inc(hc_done, 1)

            with dve.Fori(0, groups) as g:
                clamp(g, 0)
                clamp(g, 1)
                scan_q(g, 0)
                for s in range(S):
                    gate(g, s)
                    if s + 1 < S:
                        scan_q(g, s + 1)
                    if s + 2 < S:
                        clamp(g, s + 2)
                    if s > 0:
                        times_c(g, s - 1)
                    scan_h(g, s)
                times_c(g, S - 1)

        @block.scalar
        def _(act):
            def keep_front(f, i):
                kind, cb, k, p = units[i]
                act.wait_ge(front_done, f * FRONT + i + 1)
                if kind == "turn":
                    src = ps_front[i % 2][0:WIN2, 0:TW2 * CB].rearrange("p (w c) -> p w c", c=CB)
                    dst = win[cb % 2][:, :, k, p * TW2:(p + 1) * TW2].rearrange("p c w -> p w c")
                else:
                    c0 = cb * CB + k * CQ
                    src = ps_front[i % 2][0:TOK, 0:CQ * BLOCKS].rearrange("p (c i b) -> p c i b", c=CQ, i=GI)
                    dst = conv[:, :, :].rearrange("p b (i c) -> p c i b", i=GI)[:, c0:c0 + CQ, :, :]
                nc.scalar.activation(dst, src, ACT.Copy).then_inc(front_kept, 1)

            def silus(f, lo, hi):
                act.preload_act_table_set("silu_and_others")
                for r in range(lo, hi):
                    b, t = r // TILES, r % TILES
                    act.wait_ge(back_done, f * RUNS + r + 1)
                    nc.scalar.activation(xs[:, t, b * BT:(b + 1) * BT], back_banks[r % 4][:, 0:BT], ACT.Silu,
                                         bias=conv_bias[:, t:t + 1]).then_inc(xs_kept, 1)
                act.preload_act_table_set("natural_log_exp_and_others")

            def keep_xd(f, b, first=False):
                act.wait_ge(xd_done, f * BANDS + b + 1)
                if not first:
                    act.wait_ge(parts_ready, f * BANDS + b)
                nc.scalar.activation(xd[:, :], ps_prep[0][:, 0:BT], ACT.Copy).then_inc(xd_ready, 1)
                nc.scalar.activation(high[:, :], ps_prep[0][:, 0:BT], ACT.Identity,
                                     scale=low_rows[:, 0:1]).then_inc(xd_ready, 1)

            def softplus(f, b, t, late, first=False):
                n = (f * RUNS + b * TILES + t) * ZSTEPS
                bias = dt_bias[:, t:t + 1]
                if late:
                    act.wait_ge(z_step, n + 3)
                    nc.scalar.activation(z_log[:, t, :], z_log[:, t, :], ACT.Ln, bias=1.0).then_inc(z_step, 1)
                    return
                act.wait_ge(z_done, f * RUNS + b * TILES + t + 1)
                if not first:
                    act.wait_ge(delta_ready, f * RUNS + (b - 1) * TILES + t + 1)
                src = ps_prep[(1 + t) % 2][:, 0:BT]
                nc.scalar.activation(z_log[:, t, :], src, ACT.Abs, bias=bias).then_inc(z_step, 1)
                nc.scalar.activation(z_pos[:, t, :], src, ACT.Relu, bias=bias).then_inc(z_step, 1)
                act.wait_ge(z_step, n + 2)
                nc.scalar.activation(z_log[:, t, :], z_log[:, t, :], ACT.Exp, scale=-1.0).then_inc(z_step, 1)

            def exp_a(g, s, first=False):
                b, t, n = s % S // STEPS, s % STEPS // N, s % N
                if n == 0:
                    act.wait_ge(delta_ready, g * RUNS + s // N + 1)
                if not first:
                    act.wait_ge(h_done, g * S + s - DA_SLOTS + 2)
                nc.scalar.activation(d_a[s % DA_SLOTS][:, :], delta[:, t, :], ACT.Exp,
                                     scale=a_neg[:, t, n:n + 1]).then_inc(d_a_ready, 1)

            def keep_b(g, s, first=False):
                act.wait_ge(b_ready, g * S + s + 1)
                if not first:
                    act.wait_ge(u_done, g * S + s - 1)
                nc.scalar.activation(b_rows[s % 2][:, :], ps_b[s % 2][:, 0:BT], ACT.Copy).then_inc(b_kept, 1)

            def keep_y(g, r):
                act.wait_ge(y_done, g * RUNS + r + 1)
                act.wait_ge(y_stored[r % 2], (g * ((RUNS + 1 - r % 2) // 2) + r // 2 + 1) * 16)
                nc.scalar.activation(y[r % 2][:, :], ps_y[:, 0:BT], ACT.Copy).then_inc(y_kept, 1)

            def group(g, more):
                for s in range(S):
                    b, j = s // STEPS, s % STEPS
                    f, fb = next_band(g, b)
                    ahead = s + DA_SLOTS - 1
                    if more or ahead < S:
                        exp_a(g, ahead)
                    if more and s - 1 in last_piece.values():
                        keep_front(g + 1, pieces[s - 1][0])
                    if s >= N + 1 and (s - N - 1) % N == 0:
                        keep_y(g, (s - N - 1) // N)
                    if more or s + B_AHEAD < S:
                        keep_b(g, s + B_AHEAD)
                    if more or b + 1 < BANDS:
                        if j == XD_AT:
                            keep_xd(f, fb)
                        if j - 1 in Z_AT[b]:
                            softplus(f, fb, Z_AT[b].index(j - 1), True)
                        if j in Z_AT[b]:
                            softplus(f, fb, Z_AT[b].index(j), False)
                    if more and b + 1 == BANDS and j in silu_at:
                        silus(f, *silu_at[j])
                keep_y(g, RUNS - 1)

            act.preload_act_table_set("natural_log_exp_and_others")
            act.wait_ge(consts_in, CONSTS)
            nc.scalar.activation(a_neg[:, :, :], a_neg[:, :, :], ACT.Exp).then_inc(a_ready, 1)
            for i in range(FRONT):
                keep_front(0, i)
            act.wait_ge(prepared, PREPARED)
            silus(0, 0, RUNS)
            keep_xd(0, 0, True)
            for t in range(TILES):
                softplus(0, 0, t, False, True)
                softplus(0, 0, t, True, True)
            for s in range(DA_SLOTS - 1):
                exp_a(0, s, True)
            for s in range(B_AHEAD):
                keep_b(0, s, s < 2)
            if last:
                with act.Fori(0, last) as g:
                    group(g, True)
            group(last, False)

        @block.tensor
        def _(pe):
            def front_waits(f, i, first=False):
                kind, cb, k, p = units[i]
                if i < 2 and not first:
                    pe.wait_ge(xs_kept, f * RUNS)
                if kind == "turn":
                    slab = cb * GI + k
                    pe.wait_ge(slab_ready[slab % SLABS], (f * (CBS * GI // SLABS) + slab // SLABS + 1) * 16)
                    if i >= 2:
                        pe.wait_ge(front_kept, f * FRONT + i - 1)
                else:
                    n = cb * (CB // CQ) + k
                    pe.wait_ge(taps_ready[n % SLOTS2], (f * (QUNITS // SLOTS2) + n // SLOTS2 + 1) * 16)
                    pe.wait_ge(front_kept, f * FRONT + (i if k == 0 else i - 1))

            def front(i, piece):
                kind, cb, k, p = units[i]
                if kind == "turn":
                    slab = cb * GI + k
                    rows = slice(CB * (slab % SLABS), CB * (slab % SLABS) + CB)
                    pixels = xpad[rows, :, :].rearrange("p r w -> p (r w)")
                    for w in range(TW2):
                        mm = nc.tensor.transpose(ps_front[i % 2][0:WIN2, w * CB:(w + 1) * CB],
                                                 pixels[:, (p * TW2 + w) * WIN2:(p * TW2 + w + 1) * WIN2],
                                                 ident[rows, rows])
                else:
                    n = cb * (CB // CQ) + k
                    for c in range(piece * CQ // HALVES, (piece + 1) * CQ // HALVES):
                        for w in range(KT2):
                            mm = nc.tensor.matmul(
                                ps_front[i % 2][0:TOK, c * BLOCKS:(c + 1) * BLOCKS],
                                taps[n % SLOTS2][:, c, w, :],
                                win[cb % 2][:, k * CQ + c, :, w:w + IMG_BLK],
                                start=(w == 0), stop=(w == KT2 - 1))
                if kind == "turn" or piece == HALVES - 1:
                    mm.then_inc(front_done, 1)

            def back(f, r, first=False):
                b, t = r // TILES, r % TILES
                if r == 0:
                    pe.wait_ge(front_kept, (f + 1) * FRONT)
                if r == 0 and not first:
                    pe.wait_ge(z_step, (f * RUNS - 1) * ZSTEPS + 2)
                if r in (4, 5) and not first:
                    pe.wait_ge(z_step, (f * RUNS + r - 3) * ZSTEPS + 2)
                if r >= 4:
                    pe.wait_ge(xs_kept, f * RUNS + r - 3)
                for j in range(BLKS):
                    mm = nc.tensor.transpose(back_banks[r % 4][:, j * TOK:(j + 1) * TOK],
                                             conv[:, b * BLKS + j, t * 128:(t + 1) * 128], ident[0:TOK, 0:TOK])
                mm.then_inc(back_done, 1)

            def project(f, b, t, first=False):
                if t == 0 and b < 2:
                    pe.wait_ge(xs_kept, f * RUNS + (RUNS if b or first else TILES))
                if t == 0 and b > 0:
                    pe.wait_ge(z_step, (f * RUNS + (b - 1) * TILES + 1) * ZSTEPS + 2)
                mm = nc.tensor.matmul(ps_prep[0][:, 0:BT], xproj[:, t, :], xs[:, t, b * BT:(b + 1) * BT],
                                      start=(t == 0), stop=(t == TILES - 1))
                if t == TILES - 1:
                    mm.then_inc(xd_done, 1)

            def delta_rows(f, b, t):
                if t == 0:
                    pe.wait_ge(parts_ready, f * BANDS + b + 1)
                else:
                    pe.wait_ge(z_step, (f * RUNS + b * TILES + t - 1) * ZSTEPS + 2)
                bank = ps_prep[(1 + t) % 2]
                for part in range(2):
                    mm = nc.tensor.matmul(bank[:, 0:BT], dtw[part][:, t, :], parts[parts_slot(b)][:, :],
                                          start=(part == 0), stop=(part == 1))
                mm.then_inc(z_done, 1)

            def spread(bank, which, s):
                b, t, n = s // STEPS, s % STEPS // N, s % N
                rows = slice(n * XB, (n + 1) * XB)
                return nc.tensor.matmul(bank[:, 0:BT], sel[rows, which, t, :], parts[parts_slot(b)][rows, :],
                                        start=True, stop=True)

            def spread_b(g, s, first=False):
                if s % STEPS == 0:
                    pe.wait_ge(parts_ready, g * BANDS + s // STEPS + 1)
                if not first:
                    pe.wait_ge(b_kept, g * S + s - 1)
                spread(ps_b[s % 2], 0, s % S).then_inc(b_ready, 1)

            def spread_c(g, s, first=False):
                if not first:
                    pe.wait_ge(hc_done, g * S + s)
                spread(ps_c, 1, s).then_inc(c_ready, 1)

            def add_y(g, s):
                b, t, n = s // STEPS, s % STEPS // N, s % N
                r = b * TILES + t
                if n == 0:
                    pe.wait_ge(y_kept, g * RUNS + r + 1)
                    nc.tensor.matmul(ps_y[:, 0:BT], skip[:, t, :], xs[:, t, b * BT:(b + 1) * BT],
                                     start=True, stop=False)
                pe.wait_ge(hc_done, g * S + s + 1)
                mm = nc.tensor.matmul(ps_y[:, 0:BT], ident[:, :], hc[s % 2][:, :],
                                      start=False, stop=(n == N - 1))
                if n == N - 1:
                    mm.then_inc(y_done, 1)

            def group(g, more):
                for s in range(S):
                    b, j = s // STEPS, s % STEPS
                    f, fb = next_band(g, b)
                    if more and s < len(pieces) and pieces[s][1] == 0:
                        front_waits(g + 1, pieces[s][0])
                    spread_c(g, s)
                    if more or s + B_AHEAD < S:
                        spread_b(g, s + B_AHEAD)
                    if more and s < len(pieces):
                        front(*pieces[s])
                    if s > 0:
                        add_y(g, s - 1)
                    if b + 1 < BANDS:
                        if j in PROJECT_AT:
                            project(f, fb, PROJECT_AT.index(j))
                    elif more:
                        if j == XD_AT - 1:
                            for t in range(TILES):
                                project(f, fb, t)
                        for r in back_at.get(j, ()):
                            back(f, r)
                    if (more or b + 1 < BANDS) and j in DELTA_AT[b]:
                        delta_rows(f, fb, DELTA_AT[b].index(j))
                add_y(g, S - 1)

            pe.wait_ge(ident_in, 16)
            for i, piece in pieces:
                if piece == 0:
                    front_waits(0, i, True)
                front(i, piece)
            pe.wait_ge(prepared, PREPARED)
            for r in range(RUNS):
                back(0, r, True)
            for t in range(TILES):
                project(0, 0, t, True)
            for t in range(TILES):
                delta_rows(0, 0, t)
            for s in range(B_AHEAD):
                spread_b(0, s, s < 2)
            if last:
                with pe.Fori(0, last) as g:
                    group(g, True)
            group(last, False)


def banded(w, k):
    cols = W + k - 1
    kt = (ROWS + k - 1) // ROWS
    t = np.zeros((C, kt * ROWS, cols, ROWS, W), np.float32)
    for o in range(ROWS):
        for j in range(W):
            t[:, o:o + k, j:j + k, o, j] = w
    t = t.reshape(QUNITS, CQ, kt, ROWS * cols, TOK).transpose(0, 3, 1, 2, 4)
    return np.ascontiguousarray(t)


def lay_out(i):
    def rows(a):
        a = np.tile(a, (GI,) + (1,) * (a.ndim - 1))
        return np.ascontiguousarray(a.reshape((TILES, 128) + a.shape[1:]).swapaxes(0, 1))

    image, channel = np.divmod(np.arange(TILES * 128).reshape(TILES, 128), C)
    xproj = np.zeros((128, TILES, XD), np.float32)
    dtw = np.zeros((XD, TILES, 128), np.float32)
    sel = np.zeros((XD, 2, TILES, 128), np.float32)
    low_rows = np.zeros((XD, 1), np.float32)
    weights = i["L1_conv_x_proj_w"]
    for part in range(2):
        for t in range(TILES):
            for p in range(128):
                m, c = image[t, p], channel[t, p]
                for n in range(N):
                    for k in range(2):
                        row = n * XB + (2 * part + k) * GI + m
                        xproj[p, t, row] = weights[R + k * N + n, c]
                        sel[row, k, t, p] = 1
                        low_rows[row] = part
                dts = m * XB + DT0 + part * R
                xproj[p, t, dts:dts + R] = weights[:R, c]
                dtw[dts:dts + R, t, p] = i["L1_conv_dt_w"][c]
                low_rows[dts:dts + R] = part
    return {
        "x": i["x"], "t1": banded(i["L0_conv_conv_w"][:, 0], K1), "ident": np.eye(128, dtype=np.float32),
        "w1": i["L0_conv_w1"], "w2": i["L0_conv_w2"], "b1": np.ascontiguousarray(i["L0_conv_b1"].reshape(FT, 128).T), "b2": i["L0_conv_b2"],
        "ln_g": i["L0_conv_ln_g"], "ln_b": i["L0_conv_ln_b"], "ls": i["L0_conv_layer_scale"].reshape(C),
        "cb1": i["L0_conv_conv_b"],
        "t2": banded(i["L1_conv_conv_w"][:, 0], K2),
        "xproj": xproj, "dtw": dtw.reshape(XD, -1), "sel": sel.reshape(XD, -1), "low_rows": low_rows,
        "ds": rows(i["L1_conv_Ds"]), "dt_bias": rows(i["L1_conv_dt_b"]), "cb2": rows(i["L1_conv_conv_b"]),
        "a_logs": rows(i["L1_conv_A_logs"]),
    }


def program(nc, groups, a, out):
    x1 = nc.dram_tensor("x1_dram", (IMAGES * C, L), F32, kind="Internal").ap()
    layer0(nc, groups, a["x"], a["t1"], a, x1)
    layer1(nc, groups, x1, a["t2"], a, out)


def kernel(**inputs):
    import concourse.bacc as bacc
    from concourse.bass_utils import run_bass_kernel_spmd

    nc = bacc.Bacc("TRN2", target_bir_lowering=False, num_devices=1)
    arrays = {name: np.ascontiguousarray(a) for name, a in lay_out({k: np.asarray(v) for k, v in inputs.items()}).items()}
    a = {name: nc.dram_tensor(f"in_{name}_dram", v.shape, mybir.dt.from_np(v.dtype), kind="ExternalInput").ap()
         for name, v in arrays.items()}
    out = nc.dram_tensor("out_dram", (IMAGES * C, L), F32, kind="ExternalOutput").ap()
    program(nc, GROUPS, a, out)
    r = run_bass_kernel_spmd(nc, [{f"in_{name}_dram": v for name, v in arrays.items()}], core_ids=[0])
    return r.results[0]["out_dram"].reshape(IMAGES, C, H, W)
```
